# Optimizing a Trainium2 kernel written in Bass

```python
import numpy as np
import jax
import jax.numpy as jnp

def _softmax(x, axis=-1):
    return jax.nn.softmax(x, axis=axis)

def _gelu(x):
    return jax.nn.gelu(x, approximate=True)

def _silu(x):
    return jax.nn.silu(x)

def _sigmoid(x):
    return jax.nn.sigmoid(x)

def _layernorm(x, axis=-1, eps=1e-05):
    m = jnp.mean(x, axis=axis, keepdims=True)
    v = jnp.var(x, axis=axis, keepdims=True)
    return (x - m) / jnp.sqrt(v + eps)

def _scatter_add(tgt, idx, src, axis=0):
    return tgt.at[idx].add(src)

def _segment_sum(src, seg, n):
    return jax.ops.segment_sum(src, seg, n)
kernel_name = 'mk_gnn_preln_d4_gnn_r8_a6dd3f'

def setup_inputs(seed: int=0):
    np.random.seed(seed)
    _w = jnp.asarray

    def _rec_inputs():
        import jax
        import jax.numpy as jnp
        _gk = jax.random.key(seed)
        x = -0.0008691 + 1 * jax.random.normal(jax.random.fold_in(_gk, 1), (6250, 64), jnp.float32)
        src = jax.random.randint(jax.random.fold_in(_gk, 2), (200000,), 0, 6250, jnp.int32)
        dst = jnp.minimum((6250 * jax.random.uniform(jax.random.fold_in(_gk, 3), (200000,)) ** 2.0).astype(jnp.int32), 49999)
        _o = jnp.argsort(dst, stable=True)
        src = src[_o]
        dst = dst[_o]
        edge_attr_16 = 5.96457e-05 + 0.999887 * jax.random.normal(jax.random.fold_in(_gk, 12), (200000, 16), jnp.float32)
        edge_attr_32 = 0.000102155 + 1.00015 * jax.random.normal(jax.random.fold_in(_gk, 13), (200000, 32), jnp.float32)
        return (x, src, dst, edge_attr_16, edge_attr_32)
    x, src, dst, edge_attr_16, edge_attr_32 = _rec_inputs()

    def _L0_gnn_setup():
        import jax, jax.numpy as jnp
        import numpy as np
        N_NODES = 2500
        N_EDGES = 80000
        H = 64
        E_FEAT = 16
        T = 2

        def _gru_cell(a, h, W_ih, W_hh, b_ih, b_hh):
            gi = a @ W_ih.T + b_ih
            gh = h @ W_hh.T + b_hh
            i_r, i_z, i_n = jnp.split(gi, 3, axis=1)
            h_r, h_z, h_n = jnp.split(gh, 3, axis=1)
            r = jax.nn.sigmoid(i_r + h_r)
            z = jax.nn.sigmoid(i_z + h_z)
            n = jnp.tanh(i_n + r * h_n)
            return (1.0 - z) * n + z * h
        key = jax.random.key(seed)
        ks = jax.random.split(key, 10)
        hv = jax.random.normal(ks[0], (N_NODES, H), dtype=jnp.float32)
        e = jax.random.normal(ks[1], (N_EDGES, E_FEAT), dtype=jnp.float32)
        src = jax.random.randint(ks[2], (N_EDGES,), 0, N_NODES, dtype=jnp.int32)
        dst = jax.random.randint(ks[3], (N_EDGES,), 0, N_NODES, dtype=jnp.int32)
        s = 0.1
        W_msg = jax.random.normal(ks[4], (T, 2 * H + E_FEAT, 2 * H), dtype=jnp.float32) * s
        b_msg = jax.random.normal(ks[5], (T, 2 * H), dtype=jnp.float32) * s
        W_ih = jax.random.normal(ks[6], (T, 3 * H, 2 * H), dtype=jnp.float32) * s
        W_hh = jax.random.normal(ks[7], (T, 3 * H, H), dtype=jnp.float32) * s
        b_ih = jax.random.normal(ks[8], (T, 3 * H), dtype=jnp.float32) * s
        b_hh = jax.random.normal(ks[9], (T, 3 * H), dtype=jnp.float32) * s
        return {'hv': hv, 'e': e, 'src': src, 'dst': dst, 'W_msg': W_msg, 'b_msg': b_msg, 'W_ih': W_ih, 'W_hh': W_hh, 'b_ih': b_ih, 'b_hh': b_hh}
    _L0_gnn_all = _L0_gnn_setup()
    _L0_gnn_in = {k: v for k, v in _L0_gnn_all.items() if k in ('W_msg', 'b_msg', 'W_ih', 'W_hh', 'b_ih', 'b_hh')}
    del _L0_gnn_all

    def _L1_gnn_setup():
        import jax, jax.numpy as jnp
        import numpy as np
        N_NODES = 12500

        def gcn_conv(x, src, dst, W, b, n_nodes):
            h = x @ W
            deg = jax.ops.segment_sum(jnp.ones_like(src, dtype=x.dtype), dst, num_segments=n_nodes)
            dinv = jax.lax.rsqrt(deg)
            norm = dinv[src] * dinv[dst]
            msgs = h[src] * norm[:, None]
            out = jax.ops.segment_sum(msgs, dst, num_segments=n_nodes)
            return out + b
        key = jax.random.key(seed)
        k1, k2, k3, k4 = jax.random.split(key, 4)
        in_dim, hid_dim, out_dim = (64, 128, 64)
        n_edges = 200000
        x = jax.random.normal(k1, (N_NODES, in_dim), dtype=jnp.float32)
        edge_index = jax.random.randint(k2, (2, n_edges), 0, N_NODES, dtype=jnp.int64)
        W1 = jax.random.normal(k3, (in_dim, hid_dim), dtype=jnp.float32) * (1.0 / np.sqrt(in_dim))
        W2 = jax.random.normal(k4, (hid_dim, out_dim), dtype=jnp.float32) * (1.0 / np.sqrt(hid_dim))
        b1 = jnp.zeros((hid_dim,), dtype=jnp.float32)
        b2 = jnp.zeros((out_dim,), dtype=jnp.float32)
        return {'x': x, 'edge_index': edge_index, 'W1': W1, 'b1': b1, 'W2': W2, 'b2': b2}
    _L1_gnn_all = _L1_gnn_setup()
    _L1_gnn_in = {k: v for k, v in _L1_gnn_all.items() if k in ('W1', 'b1', 'W2', 'b2')}
    del _L1_gnn_all

    def _L2_gnn_setup():
        import jax, jax.numpy as jnp
        import numpy as np
        N_NODES = 12500
        N_EDGES = 200000
        IN_CH = 64
        OUT_CH = 64
        EDGE_DIM = 16
        key = jax.random.key(seed)
        ks = jax.random.split(key, 8)
        x = jax.random.normal(ks[0], (N_NODES, IN_CH), dtype=jnp.float32)
        edge_index = jax.random.randint(ks[1], (2, N_EDGES), 0, N_NODES, dtype=jnp.int64)
        edge_attr = jax.random.normal(ks[2], (N_EDGES, EDGE_DIM), dtype=jnp.float32)
        W_l = jax.random.normal(ks[3], (IN_CH, OUT_CH), dtype=jnp.float32) / np.sqrt(IN_CH)
        b_l = jnp.zeros((OUT_CH,), dtype=jnp.float32)
        W_r = jax.random.normal(ks[4], (IN_CH, OUT_CH), dtype=jnp.float32) / np.sqrt(IN_CH)
        W_e = jax.random.normal(ks[5], (EDGE_DIM, OUT_CH), dtype=jnp.float32) / np.sqrt(EDGE_DIM)
        b_e = jax.random.normal(ks[6], (OUT_CH,), dtype=jnp.float32) * 0.01
        return {'x': x, 'edge_index': edge_index, 'edge_attr': edge_attr, 'W_l': W_l, 'b_l': b_l, 'W_r': W_r, 'W_e': W_e, 'b_e': b_e}
    _L2_gnn_all = _L2_gnn_setup()
    _L2_gnn_in = {k: v for k, v in _L2_gnn_all.items() if k in ('W_l', 'b_l', 'W_r', 'W_e', 'b_e')}
    del _L2_gnn_all

    def _L3_gnn_setup():
        import jax, jax.numpy as jnp
        import numpy as np
        N_NODES = 12500
        N_EDGES = 125000
        NODE_DIM = 64
        EDGE_DIM = 32
        HIDDEN = 64

        def _unif(key, shape, fan_in):
            bound = 1.0 / np.sqrt(fan_in)
            return jax.random.uniform(key, shape, jnp.float32, -bound, bound)
        key = jax.random.key(seed)
        ks = jax.random.split(key, 11)
        node_features = jax.random.normal(ks[0], (N_NODES, NODE_DIM), jnp.float32)
        edge_index = jax.random.randint(ks[1], (2, N_EDGES), 0, N_NODES, dtype=jnp.int64)
        edge_features = jax.random.normal(ks[2], (N_EDGES, EDGE_DIM), jnp.float32)
        in_dim = 2 * NODE_DIM + EDGE_DIM
        W1 = _unif(ks[3], (HIDDEN, in_dim), in_dim)
        b1 = _unif(ks[4], (HIDDEN,), in_dim)
        W2 = _unif(ks[5], (HIDDEN, HIDDEN), HIDDEN)
        b2 = _unif(ks[6], (HIDDEN,), HIDDEN)
        w_ih = _unif(ks[7], (3 * NODE_DIM, HIDDEN), NODE_DIM)
        w_hh = _unif(ks[8], (3 * NODE_DIM, NODE_DIM), NODE_DIM)
        b_ih = _unif(ks[9], (3 * NODE_DIM,), NODE_DIM)
        b_hh = _unif(ks[10], (3 * NODE_DIM,), NODE_DIM)
        return {'node_features': node_features, 'edge_index': edge_index, 'edge_features': edge_features, 'W1': W1, 'b1': b1, 'W2': W2, 'b2': b2, 'w_ih': w_ih, 'w_hh': w_hh, 'b_ih': b_ih, 'b_hh': b_hh}
    _L3_gnn_all = _L3_gnn_setup()
    _L3_gnn_in = {k: v for k, v in _L3_gnn_all.items() if k in ('W1', 'b1', 'W2', 'b2', 'w_ih', 'w_hh', 'b_ih', 'b_hh')}
    del _L3_gnn_all
    return {'x': x, 'src': src, 'dst': dst, 'edge_attr_16': edge_attr_16, 'edge_attr_32': edge_attr_32, 'L0_gnn_W_msg': _L0_gnn_in['W_msg'], 'L0_gnn_b_msg': _L0_gnn_in['b_msg'], 'L0_gnn_W_ih': _L0_gnn_in['W_ih'], 'L0_gnn_W_hh': _L0_gnn_in['W_hh'], 'L0_gnn_b_ih': _L0_gnn_in['b_ih'], 'L0_gnn_b_hh': _L0_gnn_in['b_hh'], 'L1_gnn_W1': _L1_gnn_in['W1'], 'L1_gnn_b1': _L1_gnn_in['b1'], 'L1_gnn_W2': _L1_gnn_in['W2'], 'L1_gnn_b2': _L1_gnn_in['b2'], 'L2_gnn_W_l': _L2_gnn_in['W_l'], 'L2_gnn_b_l': _L2_gnn_in['b_l'], 'L2_gnn_W_r': _L2_gnn_in['W_r'], 'L2_gnn_W_e': _L2_gnn_in['W_e'], 'L2_gnn_b_e': _L2_gnn_in['b_e'], 'L3_gnn_W1': _L3_gnn_in['W1'], 'L3_gnn_b1': _L3_gnn_in['b1'], 'L3_gnn_W2': _L3_gnn_in['W2'], 'L3_gnn_b2': _L3_gnn_in['b2'], 'L3_gnn_w_ih': _L3_gnn_in['w_ih'], 'L3_gnn_w_hh': _L3_gnn_in['w_hh'], 'L3_gnn_b_ih': _L3_gnn_in['b_ih'], 'L3_gnn_b_hh': _L3_gnn_in['b_hh']}

def reference(x, src, dst, edge_attr_16, edge_attr_32, L0_gnn_W_msg, L0_gnn_b_msg, L0_gnn_W_ih, L0_gnn_W_hh, L0_gnn_b_ih, L0_gnn_b_hh, L1_gnn_W1, L1_gnn_b1, L1_gnn_W2, L1_gnn_b2, L2_gnn_W_l, L2_gnn_b_l, L2_gnn_W_r, L2_gnn_W_e, L2_gnn_b_e, L3_gnn_W1, L3_gnn_b1, L3_gnn_W2, L3_gnn_b2, L3_gnn_w_ih, L3_gnn_w_hh, L3_gnn_b_ih, L3_gnn_b_hh):
    import jax
    import jax.numpy as jnp

    def _L0_gnn_ref(hv, e, src, dst, W_msg, b_msg, W_ih, W_hh, b_ih, b_hh):
        import jax, jax.numpy as jnp
        import numpy as np
        N_NODES = 2500
        N_EDGES = 80000
        H = 64
        E_FEAT = 16
        T = 2

        def _gru_cell(a, h, W_ih, W_hh, b_ih, b_hh):
            gi = a @ W_ih.T + b_ih
            gh = h @ W_hh.T + b_hh
            i_r, i_z, i_n = jnp.split(gi, 3, axis=1)
            h_r, h_z, h_n = jnp.split(gh, 3, axis=1)
            r = jax.nn.sigmoid(i_r + h_r)
            z = jax.nn.sigmoid(i_z + h_z)
            n = jnp.tanh(i_n + r * h_n)
            return (1.0 - z) * n + z * h
        num_nodes = hv.shape[0]
        num_rounds = W_msg.shape[0]
        for t in range(num_rounds):
            msg_in = jnp.concatenate([hv[dst], hv[src], e], axis=1)
            msgs = msg_in @ W_msg[t] + b_msg[t]
            a = jax.ops.segment_sum(msgs, dst, num_segments=num_nodes)
            hv = _gru_cell(a, hv, W_ih[t], W_hh[t], b_ih[t], b_hh[t])
        return hv

    def _L1_gnn_ref(x, edge_index, W1, b1, W2, b2):
        import jax, jax.numpy as jnp
        import numpy as np
        N_NODES = 12500

        def gcn_conv(x, src, dst, W, b, n_nodes):
            h = x @ W
            deg = jax.ops.segment_sum(jnp.ones_like(src, dtype=x.dtype), dst, num_segments=n_nodes)
            dinv = jax.lax.rsqrt(deg)
            norm = dinv[src] * dinv[dst]
            msgs = h[src] * norm[:, None]
            out = jax.ops.segment_sum(msgs, dst, num_segments=n_nodes)
            return out + b
        n = x.shape[0]
        loops = jnp.arange(n, dtype=edge_index.dtype)
        src = jnp.concatenate([edge_index[0], loops])
        dst = jnp.concatenate([edge_index[1], loops])
        h = gcn_conv(x, src, dst, W1, b1, n)
        h = jax.nn.relu(h)
        out = gcn_conv(h, src, dst, W2, b2, n)
        return out

    def _L2_gnn_ref(x, edge_index, edge_attr, W_l, b_l, W_r, W_e, b_e):
        import jax, jax.numpy as jnp
        import numpy as np
        N_NODES = 12500
        N_EDGES = 200000
        IN_CH = 64
        OUT_CH = 64
        EDGE_DIM = 16
        N = x.shape[0]
        row, col = (edge_index[0], edge_index[1])
        x_j = x[row]
        agg = jax.ops.segment_sum(x_j, col, num_segments=N)
        cnt = jax.ops.segment_sum(jnp.ones((row.shape[0],), x.dtype), col, num_segments=N)
        mean = agg / jnp.maximum(cnt, 1.0)[:, None]
        out = mean @ W_l + b_l + x @ W_r
        e = edge_attr @ W_e + b_e
        out = out + jnp.zeros_like(out).at[col].set(e)
        return out

    def _L3_gnn_ref(node_features, edge_index, edge_features, W1, b1, W2, b2, w_ih, w_hh, b_ih, b_hh):
        import jax, jax.numpy as jnp
        import numpy as np
        N_NODES = 12500
        N_EDGES = 125000
        NODE_DIM = 64
        EDGE_DIM = 32
        HIDDEN = 64

        def _unif(key, shape, fan_in):
            bound = 1.0 / np.sqrt(fan_in)
            return jax.random.uniform(key, shape, jnp.float32, -bound, bound)
        src, dst = (edge_index[0], edge_index[1])
        x = jnp.concatenate([node_features[src], node_features[dst], edge_features], axis=-1)
        h = jax.nn.relu(x @ W1.T + b1)
        messages = h @ W2.T + b2
        agg = jax.ops.segment_sum(messages, dst, num_segments=node_features.shape[0])
        gi = agg @ w_ih.T + b_ih
        gh = node_features @ w_hh.T + b_hh
        i_r, i_z, i_n = jnp.split(gi, 3, axis=-1)
        h_r, h_z, h_n = jnp.split(gh, 3, axis=-1)
        r = jax.nn.sigmoid(i_r + h_r)
        z = jax.nn.sigmoid(i_z + h_z)
        n = jnp.tanh(i_n + r * h_n)
        return (1.0 - z) * n + z * node_features
    edge_index = jnp.stack([src, dst])
    h = jnp.maximum(_layernorm(x, axis=-1), 0.0)
    x = x + _L0_gnn_ref(h, edge_attr_16, src, dst, L0_gnn_W_msg, L0_gnn_b_msg, L0_gnn_W_ih, L0_gnn_W_hh, L0_gnn_b_ih, L0_gnn_b_hh)
    h = jnp.maximum(_layernorm(x, axis=-1), 0.0)
    x = x + _L1_gnn_ref(h, edge_index, L1_gnn_W1, L1_gnn_b1, L1_gnn_W2, L1_gnn_b2)
    h = jnp.maximum(_layernorm(x, axis=-1), 0.0)
    x = x + _L2_gnn_ref(h, edge_index, edge_attr_16, L2_gnn_W_l, L2_gnn_b_l, L2_gnn_W_r, L2_gnn_W_e, L2_gnn_b_e)
    h = jnp.maximum(_layernorm(x, axis=-1), 0.0)
    x = x + _L3_gnn_ref(h, edge_index, edge_attr_32, L3_gnn_W1, L3_gnn_b1, L3_gnn_W2, L3_gnn_b2, L3_gnn_w_ih, L3_gnn_w_hh, L3_gnn_b_ih, L3_gnn_b_hh)
    return x

_drawn_inputs = setup_inputs


def setup_inputs(seed=0):
    import zlib

    import numpy as np

    out = dict(_drawn_inputs(seed))
    spreads = {'L1_gnn_b1': (0.0, 0.1), 'L1_gnn_b2': (0.0, 0.1), 'L2_gnn_b_l': (0.0, 0.1)}
    factors = {'L0_gnn_b_ih': 2.859,
     'L0_gnn_b_hh': 2.758,
     'L2_gnn_b_e': 8.0,
     'L3_gnn_b_ih': 5.555,
     'L3_gnn_b_hh': 7.973}
    for name, (base, spread) in spreads.items():
        noise = np.random.default_rng([zlib.crc32(name.encode()), seed]).standard_normal(out[name].shape)
        drawn = base * np.exp(spread * noise) if base else spread * noise
        out[name] = jnp.asarray(drawn.astype(out[name].dtype))
    for name, factor in factors.items():
        out[name] = (out[name] * factor).astype(out[name].dtype)
    return out
```

```python
import concourse.bass as bass
from concourse import mybir
from contextlib import ExitStack

P = 128
N = 6250
E = 200000
H = 64
F16, F32 = 16, 32
NT = -(-N // P)
TB = 4
NB = -(-NT // TB)
NTP = NB * TB
CH = -(-E // P)
CHP = 13 * P
PAD_DST = 8191
GC = 4
GMAX = -(-(CH + GC) // GC)
RAW = 2 * GC
RBG = 16
RBLK = RBG * RAW
RBMAX = -(-GMAX // RBG)
EPS = 1e-5

f32 = mybir.dt.float32
i32 = mybir.dt.int32
ALU = mybir.AluOpType
ACT = mybir.ActivationFunctionType
AX = mybir.AxisListType.X
ds = bass.ds


def gnn(nc, D, out):
    with ExitStack() as ctx:
        def sb(name, shape, dt=f32):
            return ctx.enter_context(nc.sbuf_tensor(name, shape, dt))

        def ps(name, shape):
            return ctx.enter_context(nc.psum_tensor(name, shape, f32))

        def sem(name):
            return ctx.enter_context(nc.semaphore(name))

        x = sb("x", [P, NTP, H])
        h = sb("h", [P, NTP, H])
        pair = sb("pair", [P, NTP, 2 * H])
        aux = sb("aux", [P, NTP, H])
        auxT = sb("auxT", [H, NTP * P])
        q = sb("q", [P, NTP, H])
        mu = sb("mu", [P, NTP])
        rstd = sb("rstd", [P, NTP])
        dinv = sb("dinv", [P, NTP])
        rcnt = sb("rcnt", [P, NTP])
        has = sb("has", [P, NTP])
        src_i = sb("src_i", [P, CHP], i32)
        dst_i = sb("dst_i", [P, CHP], i32)
        dst_f = sb("dst_f", [P, CHP])
        tile_tab = sb("tile_tab", [1, NT + 1, 4], i32)
        rowp = sb("rowp", [1, P, 2])
        rowf = sb("rowf", [1, 4, P])
        rowi = sb("rowi", [1, 4, P], i32)
        iota_f = sb("iota_f", [P, P])
        iota_i = sb("iota_i", [P, P], i32)
        pcol_i = sb("pcol_i", [P, 1], i32)
        pcol = sb("pcol", [P, 1])
        tbase_i = sb("tbase_i", [P, NTP], i32)
        tbase = sb("tbase", [P, NTP])
        tnode = sb("tnode", [P, NTP])
        ident = sb("ident", [P, P])
        ones2 = sb("ones2", [2, P])
        zrow = sb("zrow", [1, P])
        pw = sb("pw", [P, 2])
        pw_i = sb("pw_i", [P, 4], i32)
        W = {k: sb("sb_" + k, list(a.shape)) for k, a in D.items() if k[0] == "w"}
        q_flat = q[:, :, :].rearrange("p t f -> p (t f)")
        cmin = q_flat[:, 0:CHP]
        cmax = q_flat[:, CHP:2 * CHP]
        raw = sb("raw", [P, 2 * CHP])
        cidx_i = raw[:, 0:CHP].bitcast(i32)
        cpick = raw[:, CHP:2 * CHP]
        cidx = sb("cidx", [P, CHP])
        mm13 = sb("mm13", [P, 2, 13])
        lohi = sb("lohi", [P, 8])
        rkey_i = sb("rkey_i", [P, RBLK], i32)
        rkey = sb("rkey", [P, RBLK])
        zeros = sb("zeros", [P, RBLK])
        rsel = sb("rsel", [P, RBLK])
        rexp = sb("rexp", [P, RBLK])
        rmax = sb("rmax", [P, 2])
        last_f = sb("last_f", [P, NTP])
        cidx0 = sb("cidx0", [P, RBMAX])
        chunk128 = sb("chunk128", [P, CHP])
        last_i = sb("last_i", [P, NTP], i32)
        onehot = sb("onehot", [P, GC, P])
        onehotT = sb("onehotT", [P, 2, 2 * P])
        dstrow = sb("dstrow", [P, 2, 2 * P], i32)
        e32t = sb("e32t", [F32, 2, 2 * P])
        e16g = sb("e16g", [P, GC, F16 + 1])
        idx_st = sb("idx_st", [P, GC], i32)
        gath = sb("gath", [P, GC, H])
        relu_s = sb("relu_s", [P, 2, 2 * H])
        stage = sb("stage", [P, TB, 2 * H])
        hstage = sb("hstage", [P, TB, H])
        uT = sb("uT", [P, TB * P])
        hT = sb("hT", [H, TB * P])
        aT = sb("aT", [P, TB * P])
        rz = sb("rz", [P, TB, 2 * H])
        cand = sb("cand", [P, TB, H])
        dif = sb("dif", [P, TB, H])

        ps_acc = ps("ps_acc", [P, 512])
        ps_z = [ps("ps_z0", [P, 512]), ps("ps_z1", [P, 512])]
        ps_t = ps("ps_t", [P, 512])
        ps_a = ps("ps_a", [P, 512])
        ps_g = ps("ps_g", [P, TB, 256])
        ps_m = ps("ps_m", [P, 512])

        table = nc.dram_tensor("table", (NTP * P, H), f32).ap()
        mm_dram = nc.dram_tensor("mm_dram", (2, CHP), f32).ap()
        lohi_dram = nc.dram_tensor("lohi_dram", (P, 2), f32).ap()

        s_load = sem("s_load")
        s_cst = sem("s_cst")
        s_cst2 = sem("s_cst2")
        s_mm = sem("s_mm")
        s_mmd = sem("s_mmd")
        s_mmb = sem("s_mmb")
        s_lh = sem("s_lh")
        s_lhd = sem("s_lhd")
        s_lhr = sem("s_lhr")
        s_tab = sem("s_tab")
        s_v = sem("s_v")
        s_pool = sem("s_pool")
        s_sq = sem("s_sq")
        s_sqd = sem("s_sqd")
        s_oh = sem("s_oh")
        s_seg = [sem("s_seg0"), sem("s_seg1")]
        s_e16 = sem("s_e16")
        s_e16f = sem("s_e16f")
        s_raw = sem("s_raw")
        s_rawf = sem("s_rawf")
        s_rawc = sem("s_rawc")
        s_rawz = sem("s_rawz")
        s_st = sem("s_st")
        s_stf = sem("s_stf")
        s_last = sem("s_last")
        s_lg = sem("s_lg")
        s_lgd = sem("s_lgd")
        s_hrdy = sem("s_hrdy")
        s_tw = sem("s_tw")
        s_twd = sem("s_twd")
        s_idx = sem("s_idx")
        s_g = [sem(f"s_g{j}") for j in range(GC)]
        s_gf = [sem(f"s_gf{j}") for j in range(GC)]
        s_acc = sem("s_acc")
        s_accf = sem("s_accf")
        s_dr = [sem("s_dr0"), sem("s_dr1")]
        s_drf = [sem("s_drf0"), sem("s_drf1")]
        s_et = [sem("s_et0"), sem("s_et1")]
        s_etf = [sem("s_etf0"), sem("s_etf1")]
        s_ohT = sem("s_ohT")
        s_ohTf = [sem("s_ohTf0"), sem("s_ohTf1")]
        s_z = sem("s_z")
        s_rl = sem("s_rl")
        s_rlf = [sem("s_rlf0"), sem("s_rlf1")]
        s_auxT = sem("s_auxT")
        s_stg = sem("s_stg")
        s_tp = sem("s_tp")
        s_uT = sem("s_uT")
        s_a = sem("s_a")
        s_aT = sem("s_aT")
        s_gt = sem("s_gt")
        s_rz = sem("s_rz")
        s_cd = sem("s_cd")
        s_th = sem("s_th")
        s_out = sem("s_out")

        def bc(ap2, n):
            return ap2.unsqueeze(2).broadcast_to([ap2.shape[0], ap2.shape[1], n])

        def first_chunk(eng, lo, g):
            return nc.s_assert_within(eng.snap(lo + g * GC), 0, CHP - GC, skip_runtime_bounds_check_because=
                                      "a tile's last group starts at or below chunk CH - 1")

        def load_range(eng, t, which=(0, 1)):
            lim = [(0, CH - 1), (1, GMAX), (0, NT * GMAX), (1, RBMAX)]
            return [eng.value_load(tile_tab[0:1, ds(t, 1), k], min_val=lim[k][0], max_val=lim[k][1]) for k in which]

        consts = [k for k in D if k[0] == "w"]
        n_load = 4 + len(consts)
        dst_cm = pair[:, :, :].rearrange("p t f -> p (t f)")[:, 0:13 * P].bitcast(i32)
        consts = [k for k in D if k[0] == "w"]
        n_load = 4 + len(consts)
        block = ctx.enter_context(nc.Block())

        @block.sync
        def _(sp):
            sp.dma_start(x[:, :, :], D["x_nm"].rearrange("p (t f) -> p t f", f=H)).then_inc(s_load, 16)
            sp.dma_start(src_i[:, :], D["srcT"]).then_inc(s_load, 16)
            sp.dma_start(dst_i[:, :], D["dstT"]).then_inc(s_load, 16)
            sp.dma_start(dst_cm, D["dst_lin"].rearrange("(p k) -> p k", p=P)).then_inc(s_load, 16)
            for k in consts:
                sp.dma_start(W[k][:, :], D[k]).then_inc(s_load, 16)
            sp.wait_ge(s_mm, 1)
            sp.sem_inc(s_mm, -1)
            sp.dma_start(mm_dram.rearrange("a (p k) -> p a k", p=P), mm13[:, :, :]).then_inc(s_mmd, 16)
            sp.wait_ge(s_mmd, 16)
            sp.dma_start(cmin[:, :], mm_dram[0, :].partition_broadcast(P)).then_inc(s_mmb, 16)
            sp.dma_start(cmax[:, :], mm_dram[1, :].partition_broadcast(P)).then_inc(s_mmb, 16)
            sp.wait_ge(s_lh, 1)
            sp.sem_inc(s_lh, -1)
            sp.dma_start(lohi_dram, lohi[:, 0:2]).then_inc(s_lhd, 16)
            sp.wait_ge(s_lhd, 16)
            sp.dma_start(rowp[:, :, :], lohi_dram.rearrange("(o p) a -> o p a", o=1)).then_inc(s_lhr, 16)
            sp.wait_ge(s_tab, 1)
            sp.sem_inc(s_tab, -1)
            with sp.Fori(0, NT) as t:
                lo, ng = load_range(sp, t)
                with sp.Fori(0, ng) as g:
                    c = first_chunk(sp, lo, g)
                    sp.wait_ge(s_e16f, 1)
                    sp.sem_inc(s_e16f, -1)
                    sp.dma_start(e16g[:, :, 0:F16],
                                 D["e16p"].rearrange("p (c f) -> p c f", f=F16)[:, ds(c, GC), :]
                                 ).then_inc(s_e16, 16)
            for k in range(6):
                rows = pair[:, :, H:] if k == 5 else h[:, :, :]
                sp.wait_ge(s_hrdy, 1)
                sp.sem_inc(s_hrdy, -1)
                sp.dma_start(table.rearrange("(t p) f -> p t f", p=P), rows).then_inc(s_tw, 16)
                sp.wait_ge(s_tw, 16 * (k + 1))
                sp.sem_inc(s_twd, 1)
            with sp.Fori(0, NT) as t:
                lo, ng = load_range(sp, t)
                with sp.Fori(0, ng) as g:
                    c = first_chunk(sp, lo, g)
                    for b in range(2):
                        at = (c + 2 * b) * P
                        sp.wait_ge(s_drf[b], 1)
                        sp.sem_inc(s_drf[b], -1)
                        sp.dma_start(dstrow[:, b, :], D["dst_lin"][ds(at, 2 * P)].partition_broadcast(P)
                                     ).then_inc(s_dr[b], 16)
                        sp.wait_ge(s_etf[b], 1)
                        sp.sem_inc(s_etf[b], -1)
                        sp.dma_start(e32t[:, b, :], D["e32T"][:, ds(at, 2 * P)]).then_inc(s_et[b], 16)
            sp.wait_ge(s_out, 1)
            sp.sem_inc(s_out, -1)
            sp.dma_start(out, x[:, :, :].rearrange("p t f -> p (t f)")).then_inc(s_load, 16)
            sp.wait_ge(s_load, 16 * (n_load + 1))

        @block.gpsimd
        def _(pool):
            for s in (s_e16f, s_rawf, s_stf, s_accf, *s_gf, *s_seg, *s_drf, *s_etf, *s_ohTf):
                pool.sem_inc(s, 1)
            pool.iota(iota_i[:, :], [[1, P]], base=0, channel_multiplier=0)
            pool.iota(pcol_i[:, :], [[0, 1]], base=0, channel_multiplier=1)
            pool.iota(tbase_i[:, :], [[P, NTP]], base=0, channel_multiplier=0)
            pool.iota(cidx_i[:, :], [[1, CHP]], base=1, channel_multiplier=0)
            pool.iota(rkey_i[:, :].rearrange("p (k o) -> p k o", o=2), [[P, RBLK // 2], [0, 2]], base=1, channel_multiplier=0)
            pool.memset(ident[:, :], 0.0).then_inc(s_pool, 1)
            pool.wait_ge(s_pool, 1)
            pool.sem_inc(s_pool, -1)
            pool.affine_select(out=ident[:, :], in_=ident[:, :], compare_op=ALU.not_equal, fill=1.0,
                               base=0, pattern=[[-1, P]], channel_multiplier=1)
            pool.memset(ones2[:, :], 1.0)
            pool.memset(zrow[:, :], 0.0)
            pool.memset(zeros[:, :], 0.0)
            pool.memset(e16g[:, :, F16:F16 + 1], 1.0)
            pool.memset(lohi[:, :], 0.0)
            pool.memset(aux[:, :, :], 0.0).then_inc(s_cst, 1)
            pool.wait_ge(s_last, 1)
            pool.sem_inc(s_last, -1)
            for t in range(NT):
                pool.indirect_dma_start(q[:, t, 0:F16], None, D["e16"],
                                        bass.IndirectOffsetOnAxis(ap=last_i[:, t:t + 1], axis=0)).then_inc(s_lg, 16)
            pool.wait_ge(s_lg, 16 * NT)
            pool.sem_inc(s_lgd, 1)
            pool.wait_ge(s_tab, 1)
            pool.sem_inc(s_tab, -1)
            for _ in range(6):
                pool.wait_ge(s_twd, 1)
                pool.sem_inc(s_twd, -1)
                with pool.Fori(0, NT) as t:
                    (ng,) = load_range(pool, t, (1,))
                    with pool.Fori(0, ng) as g:
                        for j in range(GC):
                            pool.wait_ge(s_idx, 1)
                            pool.sem_inc(s_idx, -1)
                            pool.indirect_dma_start(
                                gath[:, j, :], None, table,
                                bass.IndirectOffsetOnAxis(ap=idx_st[:, j:j + 1], axis=0)).then_inc(s_g[j], 16)

        @block.scalar
        def _(act):
            def norm():
                act.wait_ge(s_sq, 1)
                act.sem_inc(s_sq, -1)
                act.activation(pair[:, :, 0:H], pair[:, :, H:], ACT.Square).then_inc(s_sqd, 1)
                act.wait_ge(s_sq, 1)
                act.sem_inc(s_sq, -1)
                act.activation(rstd[:, :], rstd[:, :], ACT.Sqrt).then_inc(s_sqd, 1)

            def front(u, hh):
                act.wait_ge(s_tp, 1)
                act.sem_inc(s_tp, -1)
                if u:
                    last = act.copy(uT[:, :], ps_t[:, :])
                if hh:
                    last = act.copy(hT[:, :], ps_a[0:H, :])
                last.then_inc(s_uT, 1)

            def gru():
                with act.Fori(0, NB) as b:
                    front(True, True)
                    act.wait_ge(s_a, 1)
                    act.sem_inc(s_a, -1)
                    act.copy(aT[:, :], ps_a[:, :]).then_inc(s_aT, 1)
                    act.wait_ge(s_gt, 1)
                    act.sem_inc(s_gt, -1)
                    act.activation(rz[:, :, :], ps_g[:, :, 0:2 * H], ACT.Sigmoid).then_inc(s_rz, 1)
                    act.wait_ge(s_cd, 1)
                    act.sem_inc(s_cd, -1)
                    act.activation(cand[:, :, :], cand[:, :, :], ACT.Tanh).then_inc(s_th, 1)

            norm()
            act.wait_ge(s_tab, 1)
            act.sem_inc(s_tab, -1)
            with act.Fori(0, NT) as t:
                (ng,) = load_range(act, t, (1,))
                act.wait_ge(s_rawz, 1)
                act.sem_inc(s_rawz, -1)
                with act.Fori(0, ng) as g:
                    act.wait_ge(s_raw, 1)
                    act.sem_inc(s_raw, -1)
                    act.copy(raw[:, ds(g * RAW, RAW)], ps_z[0][:, 0:RAW]).then_inc(s_rawf, 1)
                act.drain().then_inc(s_rawc, 1)
            act.wait_ge(s_sq, 1)
            act.sem_inc(s_sq, -1)
            act.activation(dinv[:, :], dinv[:, :], ACT.Sqrt).then_inc(s_sqd, 1)
            with act.Fori(0, NB) as b:
                act.wait_ge(s_tp, 1)
                act.sem_inc(s_tp, -1)
                act.copy(auxT[:, ds(b * (TB * P), TB * P)], ps_a[0:H, :]).then_inc(s_uT, 1)
            gru()
            gru()
            norm()
            with act.Fori(0, NB) as b:
                front(True, False)
                act.wait_ge(s_a, 1)
                act.sem_inc(s_a, -1)
                act.activation(aT[:, :], ps_a[:, :], ACT.Relu, bias=W["w_b1c"][:, 0:1]).then_inc(s_aT, 1)
            norm()
            with act.Fori(0, NB) as b:
                front(True, False)
                act.wait_ge(s_a, 1)
                act.sem_inc(s_a, -1)
                act.copy(aT[0:H, :], ps_a[0:H, :]).then_inc(s_aT, 1)
            norm()
            with act.Fori(0, NB) as b:
                front(False, True)
            with act.Fori(0, NT) as t:
                (ng,) = load_range(act, t, (1,))
                with act.Fori(0, ng) as g:
                    for b in range(2):
                        act.wait_ge(s_z, 1)
                        act.sem_inc(s_z, -1)
                        act.sem_inc(s_gf[2 * b + 1], 1)
                        act.wait_ge(s_rlf[b], 1)
                        act.sem_inc(s_rlf[b], -1)
                        act.activation(relu_s[:, b, :], ps_z[b][:, 0:2 * H], ACT.Relu).then_inc(s_rl, 1)
            gru()

        @block.tensor
        def _(pe):
            zero64 = zrow[0:1, 0:H]

            def spread(k, edge_net=False):
                total = pe.value_load(tile_tab[0:1, NT:NT + 1, 2], min_val=0, max_val=NT * GMAX)
                with pe.Fori(0, NT) as t:
                    ng, before = load_range(pe, t, (1, 2))
                    pe.wait_ge(s_accf, 1)
                    pe.sem_inc(s_accf, -1)
                    pe.matmul(ps_acc[:, 0:H], zrow[0:1, :], zero64, start=True, stop=False)
                    with pe.Fori(0, ng) as g:
                        landed = pe.snap((total * k + before + g + 1) * 16)
                        if not edge_net:
                            for j in range(GC):
                                pe.wait_ge(s_oh, 1)
                                pe.sem_inc(s_oh, -1)
                                pe.wait_ge(s_g[j], landed)
                                pe.matmul(ps_acc[:, 0:H], onehot[:, j, :], gath[:, j, :],
                                          start=False, stop=False).then_inc(s_gf[j], 1)
                        else:
                            for b in range(2):
                                pe.wait_ge(s_ohT, 1)
                                pe.sem_inc(s_ohT, -1)
                                pe.sem_inc(s_drf[b], 1)
                                pe.wait_ge(s_et[b], 16)
                                pe.sem_inc(s_et[b], -16)
                                for i in range(2):
                                    zo = ps_z[b][:, i * H:(i + 1) * H]
                                    j = 2 * b + i
                                    m = pe.matmul(zo, onehotT[:, b, i * P:(i + 1) * P], q[:, ds(t, 1), :],
                                                  start=True, stop=False)
                                    if i:
                                        m.then_inc(s_ohTf[b], 1)
                                    m = pe.matmul(zo, e32t[:, b, i * P:(i + 1) * P], W["w_e3"][:, :],
                                                  start=False, stop=False)
                                    if i:
                                        m.then_inc(s_etf[b], 1)
                                    pe.wait_ge(s_g[j], landed)
                                    pe.matmul(zo, ident[:, :], gath[:, j, :], start=False,
                                              stop=True).then_inc(s_z if i else s_gf[j], 1)
                            for b in range(2):
                                pe.wait_ge(s_rl, 1)
                                pe.sem_inc(s_rl, -1)
                                for i in range(2):
                                    pe.wait_ge(s_oh, 1)
                                    pe.sem_inc(s_oh, -1)
                                    m = pe.matmul(ps_acc[:, 0:H], onehot[:, 2 * b + i, :],
                                                  relu_s[:, b, i * H:(i + 1) * H], start=False, stop=False)
                                m.then_inc(s_seg[b], 1)
                    pe.matmul(ps_acc[:, 0:H], zrow[0:1, :], zero64, start=False, stop=True).then_inc(s_acc, 1)

            def front(u, hh):
                pe.wait_ge(s_stg, 1)
                pe.sem_inc(s_stg, -1)
                if u:
                    for j in range(TB):
                        last = pe.transpose(ps_t[:, j * P:(j + 1) * P], stage[:, j, :], ident[:, :])
                if hh:
                    for j in range(TB):
                        last = pe.transpose(ps_a[0:H, j * P:(j + 1) * P], hstage[:, j, :], ident[:, :])
                last.then_inc(s_tp, 1)
                pe.wait_ge(s_uT, 1)
                pe.sem_inc(s_uT, -1)

            def gru(k):
                with pe.Fori(0, NB) as b:
                    front(True, True)
                    pe.matmul(ps_a[:, :], W[f"w_a{k}"][:, :], uT[:, :], start=True, stop=False)
                    pe.matmul(ps_a[:, :], W[f"w_x{k}"][:, :], auxT[:, ds(b * (TB * P), TB * P)],
                              start=False, stop=True).then_inc(s_a, 1)
                    pe.wait_ge(s_aT, 1)
                    pe.sem_inc(s_aT, -1)
                    for j in range(TB):
                        col = slice(j * P, (j + 1) * P)
                        pe.matmul(ps_g[:, j, :], aT[:, col], W[f"w_i{k}"][:, :], start=True, stop=False)
                        pe.matmul(ps_g[:, j, :], hT[:, col], W[f"w_h{k}"][:, :], start=False, stop=False)
                        last = pe.matmul(ps_g[:, j, :], ones2[:, :], W[f"w_b{k}"][:, :], start=False, stop=True)
                    last.then_inc(s_gt, 1)

            pe.wait_ge(s_cst2, 1)
            pe.sem_inc(s_cst2, -1)
            pe.wait_ge(s_tab, 1)
            pe.sem_inc(s_tab, -1)
            with pe.Fori(0, NT) as t:
                (ng,) = load_range(pe, t, (1,))
                pe.wait_ge(s_stf, 1)
                pe.sem_inc(s_stf, -1)
                pe.matmul(ps_m[:, 0:F16 + 1], zrow[0:1, :], zrow[0:1, 0:F16 + 1], start=True, stop=False)
                with pe.Fori(0, ng) as g:
                    pe.wait_ge(s_e16, 16)
                    pe.sem_inc(s_e16, -16)
                    pe.wait_ge(s_rawf, 1)
                    pe.sem_inc(s_rawf, -1)
                    for b in range(2):
                        for j in (2 * b, 2 * b + 1):
                            pe.wait_ge(s_oh, 1)
                            pe.sem_inc(s_oh, -1)
                            m = pe.matmul(ps_z[0][:, 2 * j:2 * j + 2], onehot[:, j, :], pw[:, :], start=True, stop=True)
                            if j == GC - 1:
                                m.then_inc(s_raw, 1)
                            m = pe.matmul(ps_m[:, 0:F16 + 1], onehot[:, j, :], e16g[:, j, :],
                                          start=False, stop=False)
                        m.then_inc(s_seg[b], 1)
                    pe.matmul(ps_m[:, 0:1], zrow[0:1, :], zrow[0:1, 0:1], start=False, stop=False).then_inc(s_e16f, 1)
                pe.matmul(ps_m[:, 0:F16 + 1], zrow[0:1, :], zrow[0:1, 0:F16 + 1], start=False, stop=True).then_inc(s_st, 1)
            with pe.Fori(0, NB) as b:
                front(False, True)
                pe.sem_inc(s_auxT, 1)
            spread(0)
            gru(0)
            spread(1)
            gru(1)
            spread(2)
            with pe.Fori(0, NB) as b:
                front(True, False)
                pe.matmul(ps_a[:, :], W["w_c1"][:, :], uT[:, :], start=True, stop=True).then_inc(s_a, 1)
                pe.wait_ge(s_aT, 1)
                pe.sem_inc(s_aT, -1)
                for j in range(TB):
                    last = pe.matmul(ps_g[:, j, 0:H], aT[:, j * P:(j + 1) * P], W["w_c2"][:, :], start=True, stop=True)
                last.then_inc(s_gt, 1)
            spread(3)
            spread(4)
            with pe.Fori(0, NB) as b:
                front(True, False)
                pe.matmul(ps_a[:, :], W["w_l"][:, :], uT[:, :], start=True, stop=False)
                pe.matmul(ps_a[:, :], W["w_le"][:, :], auxT[:, ds(b * (TB * P), TB * P)],
                          start=False, stop=True).then_inc(s_a, 1)
                pe.wait_ge(s_aT, 1)
                pe.sem_inc(s_aT, -1)
                for j in range(TB):
                    last = pe.transpose(ps_g[:, j, 0:H], aT[0:H, j * P:(j + 1) * P], ident[0:H, 0:H])
                last.then_inc(s_gt, 1)
            with pe.Fori(0, NB) as b:
                front(False, True)
                for j in range(TB):
                    pe.matmul(ps_g[:, j, 0:P], hT[:, j * P:(j + 1) * P], W["w_pq"][:, :], start=True, stop=False)
                    last = pe.matmul(ps_g[:, j, 0:P], ones2[0:1, :], W["w_bq"][:, :], start=False, stop=True)
                last.then_inc(s_gt, 1)
            spread(5, True)
            gru(2)

        @block.vector
        def _(v):
            def link(ins):
                ins.then_inc(s_v, 1)
                v.wait_ge(s_v, 1)
                v.sem_inc(s_v, -1)

            def block_of(buf, b):
                return buf[:, ds(b * TB, TB), :]

            def norm():
                link(v.reduce_sum(mu[:, :], x[:, :, :], AX))
                link(v.tensor_scalar(mu[:, :], mu[:, :], 1.0 / H, None, ALU.mult))
                v.tensor_tensor(pair[:, :, H:], x[:, :, :], bc(mu[:, :], H), ALU.subtract).then_inc(s_sq, 1)
                v.wait_ge(s_sqd, 1)
                v.sem_inc(s_sqd, -1)
                link(v.reduce_sum(rstd[:, :], pair[:, :, 0:H], AX))
                link(v.tensor_scalar(rstd[:, :], rstd[:, :], 1.0 / H, EPS, ALU.mult, ALU.add))
                v.reciprocal(rstd[:, :], rstd[:, :]).then_inc(s_sq, 1)
                v.wait_ge(s_sqd, 1)
                v.sem_inc(s_sqd, -1)
                link(v.scalar_tensor_tensor(out=h[:, :, :], in0=pair[:, :, H:], scalar=0.0,
                                            in1=bc(rstd[:, :], H), op0=ALU.max, op1=ALU.mult))
                link(v.memset(pair[:, NT:, 0:H], 0.0))

            def make_onehot(c, t, j):
                v.tensor_scalar(onehot[:, j, :], iota_f[:, :], tbase[:, ds(t, 1)], dst_f[:, ds(c + j, 1)],
                                ALU.add, ALU.is_equal).then_inc(s_oh, 1)

            def stage_idx(c, j):
                v.wait_ge(s_gf[j], 1)
                v.sem_inc(s_gf[j], -1)
                v.tensor_copy(idx_st[:, j:j + 1], src_i[:, ds(c + j, 1)]).then_inc(s_idx, 1)

            def spread(edge_net=False):
                with v.Fori(0, NT) as t:
                    lo, ng = load_range(v, t)
                    with v.Fori(0, ng) as g:
                        c = first_chunk(v, lo, g)
                        for b in range(2):
                            for j in (2 * b, 2 * b + 1):
                                stage_idx(c, j)
                                if not edge_net:
                                    make_onehot(c, t, j)
                            if edge_net:
                                v.wait_ge(s_dr[b], 16)
                                v.sem_inc(s_dr[b], -16)
                                v.wait_ge(s_ohTf[b], 1)
                                v.sem_inc(s_ohTf[b], -1)
                                v.tensor_scalar(onehotT[:, b, :], dstrow[:, b, :], tnode[:, ds(t, 1)], None,
                                                ALU.is_equal).then_inc(s_ohT, 1)
                        if edge_net:
                            for b in range(2):
                                v.wait_ge(s_seg[b], 1)
                                v.sem_inc(s_seg[b], -1)
                                v.sem_inc(s_rlf[b], 1)
                                make_onehot(c, t, 2 * b)
                                make_onehot(c, t, 2 * b + 1)
                    v.wait_ge(s_acc, 1)
                    v.sem_inc(s_acc, -1)
                    link(v.tensor_copy(pair[:, ds(t, 1), 0:H], ps_acc[:, 0:H]))
                    v.sem_inc(s_accf, 1)

            def gru(k):
                with v.Fori(0, NB) as b:
                    v.tensor_copy(stage[:, :, :], block_of(pair, b))
                    v.tensor_copy(hstage[:, :, :], block_of(h, b)).then_inc(s_stg, 1)
                    v.wait_ge(s_rz, 1)
                    v.sem_inc(s_rz, -1)
                    link(v.tensor_tensor(cand[:, :, :], rz[:, :, 0:H], ps_g[:, :, 3 * H:], ALU.mult))
                    v.tensor_tensor(cand[:, :, :], cand[:, :, :], ps_g[:, :, 2 * H:3 * H], ALU.add).then_inc(s_cd, 1)
                    v.wait_ge(s_th, 1)
                    v.sem_inc(s_th, -1)
                    link(v.tensor_tensor(dif[:, :, :], hstage[:, :, :], cand[:, :, :], ALU.subtract))
                    link(v.tensor_tensor(dif[:, :, :], dif[:, :, :], rz[:, :, H:], ALU.mult))
                    if k == 0:
                        link(v.tensor_tensor(block_of(h, b), dif[:, :, :], cand[:, :, :], ALU.add))
                    else:
                        link(v.tensor_tensor(dif[:, :, :], dif[:, :, :], cand[:, :, :], ALU.add))
                        link(v.tensor_tensor(block_of(x, b), block_of(x, b), dif[:, :, :], ALU.add))

            v.wait_ge(s_cst, 1)
            v.wait_ge(s_load, 16 * n_load)
            v.tensor_copy(iota_f[:, :], iota_i[:, :])
            v.tensor_copy(pcol[:, :], pcol_i[:, :])
            v.tensor_copy(tbase[:, :], tbase_i[:, :])
            v.tensor_copy(cidx[:, :], cidx_i[:, :])
            v.tensor_copy(rkey[:, :], rkey_i[:, :])
            v.tensor_copy(dst_f[:, :], dst_i[:, :])
            v.tensor_scalar(chunk128[:, :], cidx_i[:, :], float(P), float(-P), ALU.mult, ALU.add)
            v.tensor_scalar(cidx0[:, :], cidx_i[:, 0:RBMAX], float(P * GC * RBG), float(-P * GC * RBG), ALU.mult, ALU.add)
            link(v.tensor_copy(pw_i[:, 0:1], pcol_i[:, :]))
            link(v.tensor_scalar(pw_i[:, 2:3], pcol_i[:, :], 1, None, ALU.bitwise_and))
            link(v.tensor_copy(lohi[:, 4:5], pw_i[:, 2:3]))
            link(v.tensor_scalar(lohi[:, 5:6], pcol[:, :], float(P // 2 - 1), None, ALU.add))
            link(v.tensor_copy(pw_i[:, 3:4], lohi[:, 5:6]))
            link(v.tensor_scalar(pw_i[:, 1:2], pw_i[:, 3:4], 23, None, ALU.logical_shift_left))
            link(v.tensor_tensor(pw[:, 1:2], pw_i[:, 1:2].bitcast(f32), lohi[:, 4:5], ALU.mult))
            link(v.tensor_tensor(pw[:, 0:1], pw_i[:, 1:2].bitcast(f32), pw[:, 1:2], ALU.subtract))
            v.tensor_scalar(tnode[:, :], tbase[:, :], pcol[:, 0:1], None, ALU.add).then_inc(s_cst2, 1)
            v.tensor_reduce(mm13[:, 0, :], dst_cm.rearrange("p (k e) -> p k e", e=P), AX, ALU.min)
            v.tensor_reduce(mm13[:, 1, :], dst_cm.rearrange("p (k e) -> p k e", e=P), AX, ALU.max).then_inc(s_mm, 1)
            link(v.tensor_scalar(lohi[:, 2:3], pcol[:, :], float(P), None, ALU.mult))
            link(v.tensor_scalar(lohi[:, 3:4], lohi[:, 2:3], float(P - 1), None, ALU.add))
            v.wait_ge(s_mmb, 32)
            link(v.scalar_tensor_tensor(out=cpick[:, :], in0=cmin[:, :], scalar=lohi[:, 3:4], in1=cidx[:, :],
                                        op0=ALU.is_le, op1=ALU.mult))
            link(v.reduce_max(lohi[:, 1:2], cpick[:, :], AX))
            link(v.tensor_scalar(cidx[:, :], cidx[:, :], -1.0, float(CHP + 1), ALU.mult, ALU.add))
            link(v.scalar_tensor_tensor(out=cpick[:, :], in0=cmax[:, :], scalar=lohi[:, 2:3], in1=cidx[:, :],
                                        op0=ALU.is_ge, op1=ALU.mult))
            link(v.reduce_max(lohi[:, 0:1], cpick[:, :], AX))
            link(v.tensor_scalar(lohi[:, 0:1], lohi[:, 0:1], -1.0, float(CHP), ALU.mult, ALU.add))
            v.tensor_scalar(lohi[:, 0:1], lohi[:, 0:1], float(CH - 1), None, ALU.min).then_inc(s_lh, 1)
            v.wait_ge(s_lhr, 16)
            link(v.tensor_tensor(rowf[:, 2, :], rowp[:, :, 1], rowp[:, :, 0], ALU.subtract))
            link(v.tensor_scalar(rowf[:, 2, :], rowf[:, 2, :], 1.0, float(GC - 1), ALU.max, ALU.add))
            link(v.tensor_copy(rowi[:, 2, :], rowf[:, 2, :]))
            link(v.tensor_scalar(rowi[:, 1, :], rowi[:, 2, :], 2, None, ALU.arith_shift_right))
            link(v.tensor_copy(rowf[:, 2, :], rowi[:, 1, :]))
            link(v.tensor_scalar(rowf[:, 3, :], rowf[:, 2, :], float(RBG - 1), None, ALU.add))
            link(v.tensor_copy(rowi[:, 2, :], rowf[:, 3, :]))
            link(v.tensor_scalar(rowi[:, 3, :], rowi[:, 2, :], 4, None, ALU.arith_shift_right))
            link(v.memset(rowf[:, 1, :], 0.0))
            link(v.tensor_tensor_scan(rowf[:, 3, :], rowf[:, 2, :], rowf[:, 1, :], 0.0, ALU.add, ALU.add))
            link(v.memset(tile_tab[:, :, :], 0))
            v.tensor_copy(tile_tab[:, 0:NT, 0], rowp[:, 0:NT, 0])
            v.tensor_copy(tile_tab[:, 0:NT, 1], rowi[:, 1, 0:NT])
            v.tensor_copy(tile_tab[:, 1:NT + 1, 2], rowf[:, 3, 0:NT])
            link(v.tensor_copy(tile_tab[:, 0:NT, 3], rowi[:, 3, 0:NT]))
            v.sem_inc(s_tab, 4)
            norm()
            with v.Fori(0, NT) as t:
                lo, ng, nr = load_range(v, t, (0, 1, 3))
                with v.Fori(0, nr) as r:
                    link(v.tensor_copy(raw[:, ds(r * RBLK, RBLK)], zeros[:, :]))
                v.sem_inc(s_rawz, 1)
                with v.Fori(0, ng) as g:
                    c = first_chunk(v, lo, g)
                    for b in range(2):
                        v.wait_ge(s_seg[b], 1)
                        v.sem_inc(s_seg[b], -1)
                        make_onehot(c, t, 2 * b)
                        make_onehot(c, t, 2 * b + 1)
                v.wait_ge(s_st, 1)
                v.sem_inc(s_st, -1)
                v.tensor_copy(aux[:, ds(t, 1), 0:F16 + 1], ps_m[:, 0:F16 + 1]).then_inc(s_stf, 1)
                v.wait_ge(s_rawc, 1)
                v.sem_inc(s_rawc, -1)
                link(v.memset(rmax[:, 0:1], 0.0))
                with v.Fori(0, nr) as r:
                    link(v.tensor_scalar(rkey_i[:, :], raw[:, ds(r * RBLK, RBLK)].bitcast(i32), 23, None,
                                         ALU.logical_shift_right))
                    link(v.tensor_copy(rexp[:, :], rkey_i[:, :]))
                    link(v.tensor_tensor(rsel[:, :], rexp[:, :], rkey[:, :], ALU.add))
                    link(v.tensor_scalar(rsel[:, :], rsel[:, :], cidx0[:, ds(r, 1)], None, ALU.add))
                    link(v.scalar_tensor_tensor(out=rsel[:, :], in0=rexp[:, :], scalar=1.0,
                                                in1=rsel[:, :], op0=ALU.is_ge, op1=ALU.mult))
                    link(v.reduce_max(rmax[:, 1:2], rsel[:, :], AX))
                    link(v.tensor_tensor(rmax[:, 0:1], rmax[:, 0:1], rmax[:, 1:2], ALU.max))
                link(v.tensor_scalar(last_f[:, ds(t, 1)], rmax[:, 0:1], chunk128[:, ds(lo, 1)], float(-(P // 2)),
                                     ALU.add, ALU.add))
            deg = aux[:, :, F16]
            link(v.tensor_scalar(dinv[:, :], deg, 1.0, None, ALU.add))
            v.reciprocal(dinv[:, :], dinv[:, :]).then_inc(s_sq, 1)
            v.wait_ge(s_sqd, 1)
            v.sem_inc(s_sqd, -1)
            link(v.tensor_scalar(rcnt[:, :], deg, 1.0, None, ALU.max))
            link(v.reciprocal(rcnt[:, :], rcnt[:, :]))
            link(v.tensor_scalar(has[:, :], deg, 1.0, None, ALU.min))
            link(v.memset(last_f[:, NT:], 0.0))
            link(v.tensor_tensor(last_f[:, :], last_f[:, :], has[:, :], ALU.mult))
            link(v.tensor_scalar(last_f[:, :], last_f[:, :], 0.0, float(E - 1), ALU.max, ALU.min))
            link(v.tensor_copy(last_i[:, :], last_f[:, :]))
            v.sem_inc(s_last, 1)
            v.wait_ge(s_lgd, 1)
            v.sem_inc(s_lgd, -1)
            link(v.tensor_tensor(aux[:, :, 32:32 + F16], q[:, :, 0:F16], bc(has[:, :], F16), ALU.mult))
            link(v.tensor_copy(aux[:, :, 48:49], has[:, :].unsqueeze(2)))
            link(v.memset(aux[:, :, 49:50], 1.0))
            with v.Fori(0, NB) as b:
                v.tensor_copy(hstage[:, :, :], block_of(aux, b)).then_inc(s_stg, 1)
                v.wait_ge(s_auxT, 1)
                v.sem_inc(s_auxT, -1)
            v.sem_inc(s_hrdy, 1)
            for k in range(2):
                link(v.tensor_tensor(pair[:, :, H:], h[:, :, :], bc(deg, H), ALU.mult))
                spread()
                gru(k)
                if k == 0:
                    v.sem_inc(s_hrdy, 1)
            norm()
            link(v.tensor_tensor(h[:, :, :], h[:, :, :], bc(dinv[:, :], H), ALU.mult))
            v.sem_inc(s_hrdy, 1)
            spread()
            link(v.tensor_tensor(pair[:, :, 0:H], pair[:, :, 0:H], h[:, :, :], ALU.add))
            link(v.tensor_tensor(pair[:, :, 0:H], pair[:, :, 0:H], bc(dinv[:, :], H), ALU.mult))
            with v.Fori(0, NB) as b:
                v.tensor_copy(stage[:, :, :], block_of(pair, b)).then_inc(s_stg, 1)
                v.wait_ge(s_gt, 1)
                v.sem_inc(s_gt, -1)
                link(v.tensor_tensor(block_of(h, b), ps_g[:, :, 0:H], bc(dinv[:, ds(b * TB, TB)], H), ALU.mult))
            v.sem_inc(s_hrdy, 1)
            spread()
            link(v.tensor_tensor(pair[:, :, 0:H], pair[:, :, 0:H], h[:, :, :], ALU.add))
            link(v.tensor_tensor(pair[:, :, 0:H], pair[:, :, 0:H], bc(dinv[:, :], H), ALU.mult))
            link(v.tensor_tensor(x[:, :, :], x[:, :, :], pair[:, :, 0:H], ALU.add))
            link(v.tensor_tensor(x[:, :, :], x[:, :, :],
                                 W["w_b2r"][:, :].unsqueeze(1).broadcast_to([P, NTP, H]), ALU.add))
            norm()
            v.sem_inc(s_hrdy, 1)
            link(v.tensor_copy(pair[:, :, H:], h[:, :, :]))
            spread()
            link(v.tensor_tensor(pair[:, :, 0:H], pair[:, :, 0:H], bc(rcnt[:, :], H), ALU.mult))
            with v.Fori(0, NB) as b:
                v.tensor_copy(stage[:, :, :], block_of(pair, b)).then_inc(s_stg, 1)
                v.wait_ge(s_gt, 1)
                v.sem_inc(s_gt, -1)
                link(v.tensor_tensor(block_of(x, b), block_of(x, b), ps_g[:, :, 0:H], ALU.add))
            norm()
            with v.Fori(0, NB) as b:
                v.tensor_copy(hstage[:, :, :], block_of(h, b)).then_inc(s_stg, 1)
                v.wait_ge(s_gt, 1)
                v.sem_inc(s_gt, -1)
                v.tensor_copy(block_of(q, b), ps_g[:, :, H:2 * H])
                link(v.tensor_copy(pair[:, ds(b * TB, TB), H:], ps_g[:, :, 0:H]))
            v.sem_inc(s_hrdy, 1)
            spread(True)
            gru(2)
            v.sem_inc(s_out, 1)


def kernel(**inputs):
    import numpy as np
    import concourse.bacc as bacc
    from concourse.bass_utils import run_bass_kernel_spmd

    I = {k: np.asarray(a) for k, a in inputs.items()}

    def edges(a, pad):
        full = np.full((CHP * P,) + a.shape[1:], pad, a.dtype)
        full[:E] = a
        return full

    def put(shape, *parts):
        full = np.zeros(shape, np.float32)
        for r, c, a in parts:
            full[r:r + a.shape[0], c:c + a.shape[1]] = a
        return full

    xp = np.zeros((NTP * P, H), np.float32)
    xp[:N] = I["x"]
    src, dst = edges(I["src"], 0), edges(I["dst"], PAD_DST)
    A = {
        "x_nm": xp.reshape(NTP, P, H).transpose(1, 0, 2).reshape(P, NTP * H),
        "srcT": src.reshape(CHP, P).T, "dstT": dst.reshape(CHP, P).T, "dst_lin": dst,
        "e16": I["edge_attr_16"],
        "e16p": edges(I["edge_attr_16"], 0).reshape(CHP, P, F16).transpose(1, 0, 2).reshape(P, CHP * F16),
        "e32T": edges(I["edge_attr_32"], 0).T,
    }

    def gates(k, w_ih, w_hh, b_ih, b_hh):
        A[f"w_i{k}"] = put((P, 4 * H), (0, 0, w_ih.T))
        A[f"w_h{k}"] = put((H, 4 * H), (0, 0, w_hh.T[:, :2 * H]), (0, 3 * H, w_hh.T[:, 2 * H:]))
        A[f"w_b{k}"] = put((2, 4 * H), (0, 0, b_ih[None]), (1, 0, b_hh[None, :2 * H]), (1, 3 * H, b_hh[None, 2 * H:]))

    for k in range(2):
        w, b = I["L0_gnn_W_msg"][k], I["L0_gnn_b_msg"][k]
        A[f"w_a{k}"] = put((P, P), (0, 0, w[H:2 * H]), (H, 0, w[:H]))
        A[f"w_x{k}"] = put((H, P), (0, 0, w[2 * H:]), (F16, 0, b[None]))
        gates(k, I["L0_gnn_W_ih"][k], I["L0_gnn_W_hh"][k], I["L0_gnn_b_ih"][k], I["L0_gnn_b_hh"][k])
    A["w_c1"] = put((P, P), (0, 0, I["L1_gnn_W1"]))
    A["w_b1c"] = I["L1_gnn_b1"][:, None]
    A["w_c2"] = I["L1_gnn_W2"]
    A["w_b2r"] = np.broadcast_to(I["L1_gnn_b2"], (P, H))
    A["w_l"] = put((P, P), (0, 0, I["L2_gnn_W_l"]), (H, 0, I["L2_gnn_W_r"]))
    A["w_le"] = put((H, P), (32, 0, I["L2_gnn_W_e"]), (48, 0, I["L2_gnn_b_e"][None]), (49, 0, I["L2_gnn_b_l"][None]))
    w1 = I["L3_gnn_W1"].T
    A["w_pq"] = put((H, P), (0, 0, w1[:H]), (0, H, w1[H:2 * H]))
    A["w_bq"] = put((1, P), (0, H, I["L3_gnn_b1"][None]))
    A["w_e3"] = w1[2 * H:]
    A["w_a2"] = put((P, P), (0, 0, I["L3_gnn_W2"].T))
    A["w_x2"] = put((H, P), (F16, 0, I["L3_gnn_b2"][None]))
    gates(2, I["L3_gnn_w_ih"], I["L3_gnn_w_hh"], I["L3_gnn_b_ih"], I["L3_gnn_b_hh"])
    A = {k: np.ascontiguousarray(a) for k, a in A.items()}

    nc = bacc.Bacc("TRN2", target_bir_lowering=False, num_devices=1)
    D = {k: nc.dram_tensor("in_" + k, a.shape, mybir.dt.from_np(a.dtype), kind="ExternalInput").ap()
         for k, a in A.items()}
    out = nc.dram_tensor("out_nm", (P, NTP * H), f32, kind="ExternalOutput").ap()
    gnn(nc, D, out)
    r = run_bass_kernel_spmd(nc, [{"in_" + k: a for k, a in A.items()}], core_ids=[0])
    got = r.results[0]["out_nm"].reshape(P, NTP, H).transpose(1, 0, 2).reshape(NTP * P, H)
    return np.ascontiguousarray(got[:N])
```

```python
import concourse.bass as bass
from concourse import mybir
from contextlib import ExitStack

P = 128
N = 6250
E = 200000
H = 64
F16, F32 = 16, 32
NT = -(-N // P)
TB = 4
NB = -(-NT // TB)
NTP = NB * TB
CH = -(-E // P)
CHE = -(-(CH + 4) // 4) * 4
CHP = 13 * P
PAD_DST = 8191
GC = 4
GMAX = -(-(CH + GC) // GC)
RAW = 2 * GC
RBG = 16
RBLK = RBG * RAW
RBMAX = -(-GMAX // RBG)
EPS = 1e-5
DW = 8
WT = P // DW
NW = NT * WT
WK = 7
WP = NW // WK
WC = NT * DW
GW = 2
GWMAX = -(-(CH + GW) // GW)
TC = NT * P
E16W = F16 + 1
SCALE = 8.0
BIG_BITS = 0x40404040

f32 = mybir.dt.float32
bf16 = mybir.dt.bfloat16
f16 = mybir.dt.float16
f8 = mybir.dt.float8e4
i32 = mybir.dt.int32
ALU = mybir.AluOpType
ACT = mybir.ActivationFunctionType
AX = mybir.AxisListType.X
ds = bass.ds


def gnn(nc, D, out):
    with ExitStack() as ctx:
        def sb(name, shape, dt=f32):
            return ctx.enter_context(nc.sbuf_tensor(name, shape, dt))

        def ps(name, shape):
            return ctx.enter_context(nc.psum_tensor(name, shape, f32))

        def sem(name):
            return ctx.enter_context(nc.semaphore(name))

        arena = sb("arena", [P, CHE * E16W])
        e16a = arena[:, :].rearrange("p (c f) -> p c f", f=E16W)
        used = [0]

        def part(width):
            used[0] += width
            assert used[0] <= CHE * E16W
            return arena[:, used[0] - width:used[0]]

        def part3(n, f):
            return part(n * f).rearrange("p (n f) -> p n f", f=f)

        pair = part3(NTP, 2 * H)
        auxT = part(NTP * P)[0:H, :]
        q = part3(NTP, H)
        amat_w = [part(TC // 4) for _ in range(4)]
        amat = [a.bitcast(f8).rearrange("p (s d) -> p s d", d=P) for a in amat_w]
        ored = part(TC // 4).bitcast(i32)
        uT = part(TB * P)
        aT = part(TB * P)
        stage = part3(TB, 2 * H)
        x = sb("x", [P, NTP, H])
        x_flat = x[:, :, :].rearrange("p t f -> p (t f)")
        h = sb("h", [P, NTP, H])
        aux = h
        h_flat = h[:, :, :].rearrange("p t f -> p (t f)")
        cmin = h_flat[:, 0:CHP]
        cmax = h_flat[:, CHP:2 * CHP]
        deg = sb("deg", [P, NTP])
        mu = sb("mu", [P, NTP])
        rstd = sb("rstd", [P, NTP])
        dinv = sb("dinv", [P, NTP])
        rcnt = sb("rcnt", [P, NTP])
        has = sb("has", [P, NTP])
        src_i = sb("src_i", [P, CHP], i32)
        dst_f = sb("dst_f", [P, CHP])
        late = sb("late", [P, 2 * CHP])
        src_lo = late[:, 0:CHP]
        key = late[:, CHP:2 * CHP]
        dst_i = key.bitcast(i32)
        tile_tab = sb("tile_tab", [1, NT + 1, 4], i32)
        win_tab = x_flat[0:1, 0:2 * NW].bitcast(i32).rearrange("o (w a) -> o w a", a=2)
        flag = sb("flag", [1, 4], i32)
        iota_f = sb("iota_f", [P, P])
        iota_h = sb("iota_h", [P, WC], f16)
        wbase = x_flat[:, 2 * NW:3 * NW]
        pcol_i = sb("pcol_i", [P, 1], i32)
        pcol = sb("pcol", [P, 1])
        tbase = sb("tbase", [P, NTP])
        tnode = sb("tnode", [P, NTP])
        ident = sb("ident", [P, P])
        ones2 = sb("ones2", [2, P])
        ones_c = sb("ones_c", [P, 1])
        zrow = sb("zrow", [1, P])
        zrow_h = sb("zrow_h", [1, WC], bf16)
        zeros = sb("zeros", [P, RBLK])
        pw = sb("pw", [P, 2])
        pw_i = sb("pw_i", [P, 4], i32)
        W = {k: sb("sb_" + k, list(a.shape)) for k, a in D.items() if k[0] == "w"}
        scr = sb("scr", [P, 3 * CHP])
        hsp = scr[:, 0:NT * 3 * H // 2].bitcast(bf16).rearrange("p (t f) -> p t f", f=3 * H)
        raw = scr[:, 0:2 * CHP]
        cidx_i = scr[:, 0:CHP].bitcast(i32)
        cpick = scr[:, CHP:2 * CHP]
        cidx_f = scr[:, 0:CHP]
        cidx = scr[:, 2 * CHP:3 * CHP]
        mm13 = sb("mm13", [P, 2, 13])
        lohi = sb("lohi", [P, 8])
        wlohi = sb("wlohi", [P, WK, 2])
        wedge = sb("wedge", [P, 2, WK])
        oh_hi = sb("oh_hi", [P, 2, GW, WC], bf16)
        oh_lo = sb("oh_lo", [P, 2, GW, P], bf16)
        onehot = sb("onehot", [P, GC, P])
        oh_row = oh_hi[0:1, :, :, :].rearrange("o a b c -> o (a b c)").bitcast(f32)
        rowp = oh_row[:, 0:2 * P].rearrange("o (p a) -> o p a", a=2)
        rowf = oh_row[:, 2 * P:6 * P].rearrange("o (a p) -> o a p", p=P)
        rowi = onehot[0:1, :, :].bitcast(i32)
        cand = sb("cand", [P, TB, H])
        dif = sb("dif", [P, TB, H])
        cand_flat = cand[:, :, :].rearrange("p t f -> p (t f)")
        dif_flat = dif[:, :, :].rearrange("p t f -> p (t f)")
        roww = pair[0:1, 0:2 * NW // (2 * H) + 1, :].rearrange("o a b -> o (a b)")[:, 0:2 * NW]
        rkey_i = cand_flat[:, 0:RBLK].bitcast(i32)
        rkey = cand_flat[:, RBLK:2 * RBLK]
        rsel = dif_flat[:, 0:RBLK]
        rexp = dif_flat[:, RBLK:2 * RBLK]
        rmax = sb("rmax", [P, 2])
        last_f = sb("last_f", [P, NTP])
        cidx0 = sb("cidx0", [P, RBMAX])
        last_i = sb("last_i", [P, NTP], i32)
        lp = [0]

        def late_part(width):
            lp[0] += width
            assert lp[0] <= 2 * CHP
            return late[:, lp[0] - width:lp[0]]

        def late_part3(n, f):
            return late_part(n * f).rearrange("p (n f) -> p n f", f=f)

        onehotT = late_part3(2, 2 * P)
        dstrow = late_part3(2, 2 * P).bitcast(i32)
        e32t = late_part3(2, 2 * P)[0:F32]
        gath = late_part3(GC, H)
        relu_s = late_part3(2, 2 * H)
        idx_st = sb("idx_st", [P, GC], i32)
        hstage = late_part3(TB, H)
        hT = late_part(TB * P)[0:H, :]
        rz = late_part3(TB, 2 * H)

        ps_acc = ps("ps_acc", [P, 512])
        ps_z = [ps("ps_z0", [P, 512]), ps("ps_z1", [P, 512])]
        ps_t = ps("ps_t", [P, 512])
        ps_a = ps("ps_a", [P, 512])
        ps_g = ps("ps_g", [P, TB, 256])
        ps_d = ps_g[:, :, :].rearrange("p (b c) f -> p b (c f)", b=2)
        ps_m = ps("ps_m", [P, 512])

        table = nc.dram_tensor("table", (NTP * P, H), f32).ap()
        wlohi_dram = nc.dram_tensor("wlohi_dram", (P * WK, 2), f32).ap()
        a_dram = nc.dram_tensor("a_dram", (NT, P, TC // 4), f32).ap()
        mm_dram = nc.dram_tensor("mm_dram", (2, CHP), f32).ap()
        lohi_dram = nc.dram_tensor("lohi_dram", (P, 2), f32).ap()

        s_x = sem("s_x")
        s_load = sem("s_load")
        s_cst = sem("s_cst")
        s_cst2 = sem("s_cst2")
        s_mm = sem("s_mm")
        s_mmd = sem("s_mmd")
        s_mmb = sem("s_mmb")
        s_lh = sem("s_lh")
        s_lhd = sem("s_lhd")
        s_lhr = sem("s_lhr")
        s_tab = sem("s_tab")
        s_wl = sem("s_wl")
        s_wld = sem("s_wld")
        s_wlr = sem("s_wlr")
        s_wsem = sem("s_wsem")
        s_woh = [sem("s_woh0"), sem("s_woh1")]
        s_win = sem("s_win")
        s_winf = [sem("s_winf0"), sem("s_winf1")]
        s_at = [sem("s_at0"), sem("s_at1")]
        s_ast = [sem("s_ast0"), sem("s_ast1")]
        s_atf = [sem("s_atf0"), sem("s_atf1")]
        s_build = sem("s_build")
        s_al = [sem(f"s_al{j}") for j in range(4)]
        s_alf = [sem(f"s_alf{j}") for j in range(4)]
        s_or = sem("s_or")
        s_d = sem("s_d")
        s_df = sem("s_df")
        s_sp1 = sem("s_sp1")
        s_sp2 = sem("s_sp2")
        s_hsp = sem("s_hsp")
        s_flag0 = sem("s_flag0")
        s_flag1 = sem("s_flag1")
        s_flag = sem("s_flag")
        s_v = sem("s_v")
        s_pool = sem("s_pool")
        s_sq = sem("s_sq")
        s_sqd = sem("s_sqd")
        s_oh = sem("s_oh")
        s_seg = [sem("s_seg0"), sem("s_seg1")]
        s_e16 = sem("s_e16")
        s_e16f = sem("s_e16f")
        s_raw = sem("s_raw")
        s_rawf = sem("s_rawf")
        s_rawc = sem("s_rawc")
        s_rawz = sem("s_rawz")
        s_st = sem("s_st")
        s_st2 = sem("s_st2")
        s_stf = sem("s_stf")
        s_last = sem("s_last")
        s_lg = sem("s_lg")
        s_lgd = sem("s_lgd")
        s_hrdy = sem("s_hrdy")
        s_tw = sem("s_tw")
        s_twd = sem("s_twd")
        s_idx = sem("s_idx")
        s_g = [sem(f"s_g{j}") for j in range(GC)]
        s_gf = [sem(f"s_gf{j}") for j in range(GC)]
        s_acc = sem("s_acc")
        s_accf = sem("s_accf")
        s_dr = [sem("s_dr0"), sem("s_dr1")]
        s_drf = [sem("s_drf0"), sem("s_drf1")]
        s_et = [sem("s_et0"), sem("s_et1")]
        s_etf = [sem("s_etf0"), sem("s_etf1")]
        s_ohT = sem("s_ohT")
        s_ohTf = [sem("s_ohTf0"), sem("s_ohTf1")]
        s_z = sem("s_z")
        s_rl = sem("s_rl")
        s_rlf = [sem("s_rlf0"), sem("s_rlf1")]
        s_auxT = sem("s_auxT")
        s_stg = sem("s_stg")
        s_tp = sem("s_tp")
        s_uT = sem("s_uT")
        s_a = sem("s_a")
        s_aT = sem("s_aT")
        s_gt = sem("s_gt")
        s_rz = sem("s_rz")
        s_cd = sem("s_cd")
        s_th = sem("s_th")
        s_out = sem("s_out")

        def bc(ap2, n):
            return ap2.unsqueeze(2).broadcast_to([ap2.shape[0], ap2.shape[1], n])

        def first_chunk(eng, lo, g, size=GC):
            return nc.s_assert_within(eng.snap(lo + g * size), 0, CH - 1, skip_runtime_bounds_check_because=
                                      "a tile's last group starts at or below chunk CH - 1")

        def load_windows(eng, t, w):
            _, vals = nc.values_load_multi_w_load_instructions(
                win_tab[0:1, ds(t * WT + w * 2, 2), :].rearrange("o w a -> o (w a)"), engines=[eng.engine],
                min_val=0, max_val=CH, skip_runtime_bounds_check_because="chunk numbers and counts")
            lo0, ng0, lo1, ng1 = vals
            bound = [(lo0, 0, CH - 1), (ng0, 1, GWMAX), (lo1, 0, CH - 1), (ng1, 1, GWMAX)]
            return [nc.s_assert_within(v, a, b, skip_runtime_bounds_check_because="the search bounds it")
                    for v, a, b in bound]

        def load_range(eng, t, which=(0, 1)):
            lim = [(0, CH - 1), (1, GMAX), (0, NT * GMAX), (1, RBMAX)]
            return [eng.value_load(tile_tab[0:1, ds(t, 1), k], min_val=lim[k][0], max_val=lim[k][1]) for k in which]

        consts = [k for k in D if k[0] == "w"]
        n_load = 3 + len(consts)
        dst_cm = arena[:, 0:13 * P].bitcast(i32)
        consts = [k for k in D if k[0] == "w"]
        n_load = 3 + len(consts)
        SPLIT = [(0, 13), (13, 26), (26, 39), (39, NT)]
        block = ctx.enter_context(nc.Block())

        @block.sync
        def _(sp):
            sp.dma_start(src_i[:, :], D["srcT"]).then_inc(s_load, 16)
            sp.dma_start(dst_i[:, :], D["dstT"]).then_inc(s_load, 16)
            sp.dma_start(dst_cm, D["dst_lin"].rearrange("(p k) -> p k", p=P)).then_inc(s_load, 16)
            for k in consts:
                sp.dma_start(W[k][:, :], D[k]).then_inc(s_load, 16)
            sp.wait_ge(s_mm, 1)
            sp.sem_inc(s_mm, -1)
            sp.dma_start(arena[:, :], D["e16p"]).then_inc(s_e16, 16)
            sp.dma_start(mm_dram.rearrange("a (p k) -> p a k", p=P), mm13[:, :, :]).then_inc(s_mmd, 16)
            sp.wait_ge(s_mmd, 16)
            sp.dma_start(cmin, mm_dram[0, :].partition_broadcast(P)).then_inc(s_mmb, 16)
            sp.dma_start(cmax, mm_dram[1, :].partition_broadcast(P)).then_inc(s_mmb, 16)
            sp.wait_ge(s_lh, 1)
            sp.sem_inc(s_lh, -1)
            sp.dma_start(lohi_dram, lohi[:, 0:2]).then_inc(s_lhd, 16)
            sp.wait_ge(s_lhd, 16)
            sp.dma_start(rowp[:, :, :], lohi_dram.rearrange("(o p) a -> o p a", o=1)).then_inc(s_lhr, 16)
            sp.wait_ge(s_tab, 1)
            sp.sem_inc(s_tab, -1)
            sp.wait_ge(s_wl, 1)
            sp.sem_inc(s_wl, -1)
            sp.dma_start(wlohi_dram.rearrange("(p k) a -> p k a", k=WK), wlohi[:, :, :]).then_inc(s_wld, 16)
            sp.wait_ge(s_wld, 16)
            sp.wait_ge(s_st2, 1)
            sp.sem_inc(s_st2, -1)
            sp.dma_start(roww, wlohi_dram[0:NW, :].rearrange("(o w) a -> o (w a)", o=1)).then_inc(s_wlr, 16)
            def store(t, b):
                sp.wait_ge(s_at[b], 1)
                sp.sem_inc(s_at[b], -1)
                sp.dma_start(a_dram[ds(t, 1), :, :].rearrange("o p c -> p (o c)"), amat_w[b]).then_inc(s_ast[b], 16)

            def stored(b):
                sp.wait_ge(s_ast[b], 16)
                sp.sem_inc(s_ast[b], -16)
                sp.sem_inc(s_atf[b], 1)

            with sp.Fori(0, NT // 2) as i:
                store(i * 2, 0)
                store(i * 2 + 1, 1)
                stored(0)
                stored(1)
            store(NT - 1, 0)
            stored(0)
            sp.dma_start(x[:, :, :], D["x_nm"].rearrange("p (t f) -> p t f", f=H)).then_inc(s_x, 16)

            def load_tile(t, b):
                sp.wait_ge(s_alf[b], 1)
                sp.sem_inc(s_alf[b], -1)
                sp.dma_start(amat_w[b], a_dram[ds(t, 1), :, :].rearrange("o p c -> p (o c)")).then_inc(s_al[b], 16)

            def dense():
                with sp.Fori(0, NT // 4) as i:
                    for b in range(4):
                        load_tile(i * 4 + b, b)
                load_tile(NT - 1, 0)

            def write_table(rows):
                sp.dma_start(table.rearrange("(t p) f -> p t f", p=P), rows).then_inc(s_tw, 16)
                sp.wait_ge(s_tw, 16)
                sp.sem_inc(s_tw, -16)
                sp.sem_inc(s_twd, 1)

            dense()
            sp.wait_ge(s_flag, 1)
            sp.sem_inc(s_flag, -1)
            big = sp.value_load(flag[0:1, 0:1], min_val=0, max_val=1)
            sp.wait_ge(s_hrdy, 1)
            sp.sem_inc(s_hrdy, -1)
            with sp.If(big):
                write_table(h[:, :, :])
            for k in range(1, 5):
                sp.wait_ge(s_hrdy, 1)
                sp.sem_inc(s_hrdy, -1)
                with sp.If(big):
                    write_table(h[:, :, :])
                with sp.Else():
                    dense()
            sp.wait_ge(s_hrdy, 1)
            sp.sem_inc(s_hrdy, -1)
            write_table(pair[:, :, H:])
            with sp.Fori(0, NT) as t:
                lo, ng = load_range(sp, t)
                with sp.Fori(0, ng) as g:
                    c = first_chunk(sp, lo, g)
                    for b in range(2):
                        at = (c + 2 * b) * P
                        sp.wait_ge(s_drf[b], 1)
                        sp.sem_inc(s_drf[b], -1)
                        sp.dma_start(dstrow[:, b, :], D["dst_lin"][ds(at, 2 * P)].partition_broadcast(P)
                                     ).then_inc(s_dr[b], 16)
                        sp.wait_ge(s_etf[b], 1)
                        sp.sem_inc(s_etf[b], -1)
                        sp.dma_start(e32t[:, b, :], D["e32T"][:, ds(at, 2 * P)]).then_inc(s_et[b], 16)
            sp.wait_ge(s_out, 1)
            sp.sem_inc(s_out, -1)
            sp.dma_start(out, x[:, :, :].rearrange("p t f -> p (t f)")).then_inc(s_load, 16)
            sp.wait_ge(s_load, 16 * (n_load + 1))

        @block.gpsimd
        def _(pool):
            for s in (s_rawf, s_stf, s_accf, s_df, *s_gf, *s_seg, *s_drf, *s_etf, *s_ohTf, *s_woh, *s_winf, *s_atf, *s_alf):
                pool.sem_inc(s, 1)
            pool.sem_inc(s_df, 1)
            pool.iota(pcol_i[:, :], [[0, 1]], base=0, channel_multiplier=1)
            pool.iota(cidx_i, [[1, CHP]], base=1, channel_multiplier=0)
            pool.iota(rkey_i.rearrange("p (k o) -> p k o", o=2), [[P, RBLK // 2], [0, 2]], base=1, channel_multiplier=0)
            pool.memset(ident[:, :], 0.0).then_inc(s_pool, 1)
            pool.wait_ge(s_pool, 1)
            pool.sem_inc(s_pool, -1)
            pool.affine_select(out=ident[:, :], in_=ident[:, :], compare_op=ALU.not_equal, fill=1.0,
                               base=0, pattern=[[-1, P]], channel_multiplier=1)
            pool.memset(ones2[:, :], 1.0)
            pool.memset(zrow[:, :], 0.0)
            pool.memset(zeros[:, :], 0.0)
            pool.memset(zrow_h[:, :], 0.0)
            pool.memset(ones_c[:, :], 1.0)
            pool.memset(flag[:, :], 0)
            pool.memset(lohi[:, :], 0.0).then_inc(s_cst, 1)
            pool.wait_ge(s_last, 1)
            pool.sem_inc(s_last, -1)
            for t in range(NT):
                pool.indirect_dma_start(q[:, t, 0:F16], None, D["e16"],
                                        bass.IndirectOffsetOnAxis(ap=last_i[:, t:t + 1], axis=0)).then_inc(s_lg, 16)
            pool.wait_ge(s_lg, 16 * NT)
            pool.sem_inc(s_lgd, 1)
            pool.wait_ge(s_tab, 1)
            pool.sem_inc(s_tab, -1)

            def spread():
                pool.wait_ge(s_twd, 1)
                pool.sem_inc(s_twd, -1)
                with pool.Fori(0, NT) as t:
                    (ng,) = load_range(pool, t, (1,))
                    with pool.Fori(0, ng) as g:
                        for j in range(GC):
                            pool.wait_ge(s_idx, 1)
                            pool.sem_inc(s_idx, -1)
                            pool.indirect_dma_start(
                                gath[:, j, :], None, table,
                                bass.IndirectOffsetOnAxis(ap=idx_st[:, j:j + 1], axis=0)).then_inc(s_g[j], 16)

            pool.wait_ge(s_flag, 1)
            pool.sem_inc(s_flag, -1)
            big = pool.value_load(flag[0:1, 0:1], min_val=0, max_val=1)
            with pool.If(big):
                with pool.Fori(0, 5) as k:
                    spread()
            spread()

        @block.scalar
        def _(act):
            def norm():
                act.wait_ge(s_sq, 1)
                act.sem_inc(s_sq, -1)
                act.activation(pair[:, :, 0:H], pair[:, :, H:], ACT.Square).then_inc(s_sqd, 1)
                act.wait_ge(s_sq, 1)
                act.sem_inc(s_sq, -1)
                act.activation(rstd[:, :], rstd[:, :], ACT.Sqrt).then_inc(s_sqd, 1)

            def front(u, hh):
                act.wait_ge(s_tp, 1)
                act.sem_inc(s_tp, -1)
                if u:
                    last = act.copy(uT[:, :], ps_t[:, :])
                if hh:
                    last = act.copy(hT[:, :], ps_a[0:H, :])
                last.then_inc(s_uT, 1)

            def gru():
                act.preload_act_table(ACT.Sigmoid)
                with act.Fori(0, NB) as b:
                    front(True, True)
                    act.wait_ge(s_a, 1)
                    act.sem_inc(s_a, -1)
                    act.copy(aT[:, :], ps_a[:, :]).then_inc(s_aT, 1)
                    act.wait_ge(s_gt, 1)
                    act.sem_inc(s_gt, -1)
                    act.activation(rz[:, :, :], ps_g[:, :, 0:2 * H], ACT.Sigmoid).then_inc(s_rz, 1)
                    act.wait_ge(s_cd, 1)
                    act.sem_inc(s_cd, -1)
                    act.activation(cand[:, :, :], cand[:, :, :], ACT.Tanh).then_inc(s_th, 1)

            def split():
                for i in range(len(SPLIT)):
                    t0, t1 = SPLIT[i]
                    if i == 0:
                        act.wait_ge(s_sp1, 1)
                        act.sem_inc(s_sp1, -1)
                    act.activation(hsp[:, t0:t1, 0:H], h[:, t0:t1, :], ACT.Copy, scale=SCALE).then_inc(s_sp2, 1)
                for p in (1, 2):
                    for t0, t1 in SPLIT:
                        act.wait_ge(s_sp1, 1)
                        act.sem_inc(s_sp1, -1)
                        act.activation(hsp[:, t0:t1, p * H:(p + 1) * H], q[:, t0:t1, :], ACT.Copy).then_inc(s_sp2, 1)

            act.preload_act_table(ACT.Copy)
            act.wait_ge(s_tab, 1)
            act.sem_inc(s_tab, -1)
            with act.Fori(0, NT) as t:
                (ng,) = load_range(act, t, (1,))
                act.wait_ge(s_rawz, 1)
                act.sem_inc(s_rawz, -1)
                with act.Fori(0, ng) as g:
                    act.wait_ge(s_raw, 1)
                    act.sem_inc(s_raw, -1)
                    act.copy(raw[:, ds(g * RAW, RAW)], ps_z[0][:, 0:RAW]).then_inc(s_rawf, 1)
                act.drain().then_inc(s_rawc, 1)
            act.wait_ge(s_sq, 1)
            act.sem_inc(s_sq, -1)
            act.activation(dinv[:, :], dinv[:, :], ACT.Sqrt).then_inc(s_sqd, 1)
            act.preload_act_table(ACT.Copy)

            def build_tile(b):
                act.wait_ge(s_atf[b], 1)
                act.sem_inc(s_atf[b], -1)
                for w in range(WT):
                    act.wait_ge(s_win, 1)
                    act.sem_inc(s_win, -1)
                    act.activation(amat[b][:, :, w * DW:(w + 1) * DW],
                                   ps_z[w % 2][:, 0:WC].rearrange("p (s d) -> p s d", d=DW), ACT.Copy,
                                   scale=1.0 / SCALE, saturate=False).then_inc(s_winf[w % 2], 1)
                act.drain().then_inc(s_at[b], 1)

            with act.Fori(0, NT // 2) as i:
                build_tile(0)
                build_tile(1)
            build_tile(0)
            with act.Fori(0, NB) as b:
                act.wait_ge(s_tp, 1)
                act.sem_inc(s_tp, -1)
                act.copy(auxT[:, ds(b * (TB * P), TB * P)], ps_a[0:H, :]).then_inc(s_uT, 1)
            norm()
            split()
            gru()
            act.wait_ge(s_flag, 1)
            act.sem_inc(s_flag, -1)
            big = act.value_load(flag[0:1, 0:1], min_val=0, max_val=1)

            def split_if_small():
                with act.If(big):
                    pass
                with act.Else():
                    split()

            split_if_small()
            gru()
            norm()
            split_if_small()
            with act.Fori(0, NB) as b:
                front(True, False)
                act.wait_ge(s_a, 1)
                act.sem_inc(s_a, -1)
                act.activation(aT[:, :], ps_a[:, :], ACT.Relu, bias=W["w_b1c"][:, 0:1]).then_inc(s_aT, 1)
            split_if_small()
            norm()
            split_if_small()
            with act.Fori(0, NB) as b:
                front(True, False)
                act.wait_ge(s_a, 1)
                act.sem_inc(s_a, -1)
                act.copy(aT[0:H, :], ps_a[0:H, :]).then_inc(s_aT, 1)
            norm()
            with act.Fori(0, NB) as b:
                front(False, True)
            with act.Fori(0, NT) as t:
                (ng,) = load_range(act, t, (1,))
                with act.Fori(0, ng) as g:
                    for b in range(2):
                        act.wait_ge(s_z, 1)
                        act.sem_inc(s_z, -1)
                        act.sem_inc(s_gf[2 * b + 1], 1)
                        act.wait_ge(s_rlf[b], 1)
                        act.sem_inc(s_rlf[b], -1)
                        act.activation(relu_s[:, b, :], ps_z[b][:, 0:2 * H], ACT.Relu).then_inc(s_rl, 1)
            gru()

        @block.tensor
        def _(pe):
            zero64 = zrow[0:1, 0:H]

            def spread(k, edge_net=False):
                total = pe.value_load(tile_tab[0:1, NT:NT + 1, 2], min_val=0, max_val=NT * GMAX)
                first = pe.snap(total * k * big)
                with pe.Fori(0, NT) as t:
                    ng, before = load_range(pe, t, (1, 2))
                    pe.wait_ge(s_accf, 1)
                    pe.sem_inc(s_accf, -1)
                    pe.matmul(ps_acc[:, 0:H], zrow[0:1, :], zero64, start=True, stop=False)
                    with pe.Fori(0, ng) as g:
                        landed = pe.snap((first + before + g + 1) * 16)
                        if not edge_net:
                            for j in range(GC):
                                pe.wait_ge(s_oh, 1)
                                pe.sem_inc(s_oh, -1)
                                pe.wait_ge(s_g[j], landed)
                                pe.matmul(ps_acc[:, 0:H], onehot[:, j, :], gath[:, j, :],
                                          start=False, stop=False).then_inc(s_gf[j], 1)
                        else:
                            for b in range(2):
                                pe.wait_ge(s_ohT, 1)
                                pe.sem_inc(s_ohT, -1)
                                pe.sem_inc(s_drf[b], 1)
                                pe.wait_ge(s_et[b], 16)
                                pe.sem_inc(s_et[b], -16)
                                for i in range(2):
                                    zo = ps_z[b][:, i * H:(i + 1) * H]
                                    j = 2 * b + i
                                    m = pe.matmul(zo, onehotT[:, b, i * P:(i + 1) * P], q[:, ds(t, 1), :],
                                                  start=True, stop=False)
                                    if i:
                                        m.then_inc(s_ohTf[b], 1)
                                    m = pe.matmul(zo, e32t[:, b, i * P:(i + 1) * P], W["w_e3"][:, :],
                                                  start=False, stop=False)
                                    if i:
                                        m.then_inc(s_etf[b], 1)
                                    pe.wait_ge(s_g[j], landed)
                                    pe.matmul(zo, ident[:, :], gath[:, j, :], start=False,
                                              stop=True).then_inc(s_z if i else s_gf[j], 1)
                            for b in range(2):
                                pe.wait_ge(s_rl, 1)
                                pe.sem_inc(s_rl, -1)
                                for i in range(2):
                                    pe.wait_ge(s_oh, 1)
                                    pe.sem_inc(s_oh, -1)
                                    m = pe.matmul(ps_acc[:, 0:H], onehot[:, 2 * b + i, :],
                                                  relu_s[:, b, i * H:(i + 1) * H], start=False, stop=False)
                                m.then_inc(s_seg[b], 1)
                    pe.matmul(ps_acc[:, 0:H], zrow[0:1, :], zero64, start=False, stop=True).then_inc(s_acc, 1)

            def front(u, hh):
                pe.wait_ge(s_stg, 1)
                pe.sem_inc(s_stg, -1)
                if u:
                    for j in range(TB):
                        last = pe.transpose(ps_t[:, j * P:(j + 1) * P], stage[:, j, :], ident[:, :])
                if hh:
                    for j in range(TB):
                        last = pe.transpose(ps_a[0:H, j * P:(j + 1) * P], hstage[:, j, :], ident[:, :])
                last.then_inc(s_tp, 1)
                pe.wait_ge(s_uT, 1)
                pe.sem_inc(s_uT, -1)

            def gru(k):
                with pe.Fori(0, NB) as b:
                    front(True, True)
                    pe.matmul(ps_a[:, :], W[f"w_a{k}"][:, :], uT[:, :], start=True, stop=False)
                    pe.matmul(ps_a[:, :], W[f"w_x{k}"][:, :], auxT[:, ds(b * (TB * P), TB * P)],
                              start=False, stop=True).then_inc(s_a, 1)
                    pe.wait_ge(s_aT, 1)
                    pe.sem_inc(s_aT, -1)
                    for j in range(TB):
                        col = slice(j * P, (j + 1) * P)
                        pe.matmul(ps_g[:, j, :], aT[:, col], W[f"w_i{k}"][:, :], start=True, stop=False)
                        pe.matmul(ps_g[:, j, :], hT[:, col], W[f"w_h{k}"][:, :], start=False, stop=False)
                        last = pe.matmul(ps_g[:, j, :], ones2[:, :], W[f"w_b{k}"][:, :], start=False, stop=True)
                    last.then_inc(s_gt, 1)

            def dense():
                pe.wait_ge(s_hsp, 1)
                pe.sem_inc(s_hsp, -1)

                def tile(b):
                    pe.wait_ge(s_al[b], 16)
                    pe.sem_inc(s_al[b], -16)
                    pe.wait_ge(s_df, 1)
                    pe.sem_inc(s_df, -1)
                    for i in range(NT):
                        last = pe.matmul(ps_d[:, b % 2, 0:3 * H], amat[b][:, i, :], hsp[:, i, :],
                                         start=(i == 0), stop=(i == NT - 1))
                    last.then_inc(s_d, 1)

                with pe.Fori(0, NT // 4) as i:
                    for b in range(4):
                        tile(b)
                tile(0)

            def build_tile(t):
                with pe.Fori(0, WT // 2) as w:
                    lo0, ng0, lo1, ng1 = load_windows(pe, t, w)
                    for i, ng in ((0, ng0), (1, ng1)):
                        pe.wait_ge(s_winf[i], 1)
                        pe.sem_inc(s_winf[i], -1)
                        pe.matmul(ps_z[i][:, 0:WC], zrow_h[0:1, 0:P], zrow_h[:, :], start=True, stop=False)
                        with pe.Fori(0, ng) as g:
                            pe.wait_ge(s_wsem, 1)
                            pe.sem_inc(s_wsem, -1)
                            for j in range(GW):
                                last = pe.matmul(ps_z[i][:, 0:WC], oh_lo[:, i, j, :], oh_hi[:, i, j, :],
                                                 start=False, stop=False)
                            last.then_inc(s_woh[i], 1)
                        pe.matmul(ps_z[i][:, 0:WC], zrow_h[0:1, 0:P], zrow_h[:, :], start=False,
                                  stop=True).then_inc(s_win, 1)

            pe.wait_ge(s_cst2, 1)
            pe.sem_inc(s_cst2, -1)
            pe.wait_ge(s_tab, 1)
            pe.sem_inc(s_tab, -1)
            pe.wait_ge(s_e16, 16)
            with pe.Fori(0, NT) as t:
                lo, ng = load_range(pe, t)
                pe.wait_ge(s_stf, 1)
                pe.sem_inc(s_stf, -1)
                pe.matmul(ps_m[:, 0:E16W], zrow[0:1, :], zrow[0:1, 0:E16W], start=True, stop=False)
                with pe.Fori(0, ng) as g:
                    c = first_chunk(pe, lo, g)
                    pe.wait_ge(s_rawf, 1)
                    pe.sem_inc(s_rawf, -1)
                    for b in range(2):
                        for j in (2 * b, 2 * b + 1):
                            pe.wait_ge(s_oh, 1)
                            pe.sem_inc(s_oh, -1)
                            m = pe.matmul(ps_z[0][:, 2 * j:2 * j + 2], onehot[:, j, :], pw[:, :], start=True, stop=True)
                            if j == GC - 1:
                                m.then_inc(s_raw, 1)
                            m = pe.matmul(ps_m[:, 0:E16W], onehot[:, j, :], e16a[:, ds(c + j, 1), :],
                                          start=False, stop=False)
                        m.then_inc(s_seg[b], 1)
                pe.matmul(ps_m[:, 0:E16W], zrow[0:1, :], zrow[0:1, 0:E16W], start=False, stop=True).then_inc(s_st, 1)
            pe.wait_ge(s_build, 1)
            pe.sem_inc(s_build, -1)
            with pe.Fori(0, NT) as t:
                build_tile(t)
            with pe.Fori(0, NB) as b:
                front(False, True)
                pe.sem_inc(s_auxT, 1)
            dense()
            pe.wait_ge(s_or, 1)
            pe.sem_inc(s_or, -1)
            pe.matmul(ps_m[0:1, 0:1], ones_c[:, :], lohi[:, 7:8], start=True, stop=True).then_inc(s_flag1, 1)
            pe.wait_ge(s_flag, 1)
            pe.sem_inc(s_flag, -1)
            big = pe.value_load(flag[0:1, 0:1], min_val=0, max_val=1)
            with pe.If(big):
                spread(0)
            gru(0)

            def in_sums(k):
                with pe.If(big):
                    spread(k)
                with pe.Else():
                    dense()

            in_sums(1)
            gru(1)
            in_sums(2)
            with pe.Fori(0, NB) as b:
                front(True, False)
                pe.matmul(ps_a[:, :], W["w_c1"][:, :], uT[:, :], start=True, stop=True).then_inc(s_a, 1)
                pe.wait_ge(s_aT, 1)
                pe.sem_inc(s_aT, -1)
                for j in range(TB):
                    last = pe.matmul(ps_g[:, j, 0:H], aT[:, j * P:(j + 1) * P], W["w_c2"][:, :], start=True, stop=True)
                last.then_inc(s_gt, 1)
            in_sums(3)
            in_sums(4)
            with pe.Fori(0, NB) as b:
                front(True, False)
                pe.matmul(ps_a[:, :], W["w_l"][:, :], uT[:, :], start=True, stop=False)
                pe.matmul(ps_a[:, :], W["w_le"][:, :], auxT[:, ds(b * (TB * P), TB * P)],
                          start=False, stop=True).then_inc(s_a, 1)
                pe.wait_ge(s_aT, 1)
                pe.sem_inc(s_aT, -1)
                for j in range(TB):
                    last = pe.transpose(ps_g[:, j, 0:H], aT[0:H, j * P:(j + 1) * P], ident[0:H, 0:H])
                last.then_inc(s_gt, 1)
            with pe.Fori(0, NB) as b:
                front(False, True)
                for j in range(TB):
                    pe.matmul(ps_g[:, j, 0:P], hT[:, j * P:(j + 1) * P], W["w_pq"][:, :], start=True, stop=False)
                    last = pe.matmul(ps_g[:, j, 0:P], ones2[0:1, :], W["w_bq"][:, :], start=False, stop=True)
                last.then_inc(s_gt, 1)
            spread(5, True)
            gru(2)

        @block.vector
        def _(v):
            def link(ins):
                ins.then_inc(s_v, 1)
                v.wait_ge(s_v, 1)
                v.sem_inc(s_v, -1)

            def block_of(buf, b):
                return buf[:, ds(b * TB, TB), :]

            def norm():
                link(v.reduce_sum(mu[:, :], x[:, :, :], AX))
                link(v.tensor_scalar(mu[:, :], mu[:, :], 1.0 / H, None, ALU.mult))
                v.tensor_tensor(pair[:, :, H:], x[:, :, :], bc(mu[:, :], H), ALU.subtract).then_inc(s_sq, 1)
                v.wait_ge(s_sqd, 1)
                v.sem_inc(s_sqd, -1)
                link(v.reduce_sum(rstd[:, :], pair[:, :, 0:H], AX))
                link(v.tensor_scalar(rstd[:, :], rstd[:, :], 1.0 / H, EPS, ALU.mult, ALU.add))
                v.reciprocal(rstd[:, :], rstd[:, :]).then_inc(s_sq, 1)
                v.wait_ge(s_sqd, 1)
                v.sem_inc(s_sqd, -1)
                link(v.scalar_tensor_tensor(out=h[:, :, :], in0=pair[:, :, H:], scalar=0.0,
                                            in1=bc(rstd[:, :], H), op0=ALU.max, op1=ALU.mult))
                link(v.memset(pair[:, NT:, 0:H], 0.0))

            def make_onehot(c, t, j):
                v.tensor_scalar(onehot[:, j, :], iota_f[:, :], tbase[:, ds(t, 1)], dst_f[:, ds(c + j, 1)],
                                ALU.add, ALU.is_equal).then_inc(s_oh, 1)

            def stage_idx(c, j):
                v.wait_ge(s_gf[j], 1)
                v.sem_inc(s_gf[j], -1)
                v.tensor_copy(idx_st[:, j:j + 1], src_i[:, ds(c + j, 1)]).then_inc(s_idx, 1)

            def spread(edge_net=False):
                with v.Fori(0, NT) as t:
                    lo, ng = load_range(v, t)
                    with v.Fori(0, ng) as g:
                        c = first_chunk(v, lo, g)
                        for b in range(2):
                            for j in (2 * b, 2 * b + 1):
                                stage_idx(c, j)
                                if not edge_net:
                                    make_onehot(c, t, j)
                            if edge_net:
                                v.wait_ge(s_dr[b], 16)
                                v.sem_inc(s_dr[b], -16)
                                v.wait_ge(s_ohTf[b], 1)
                                v.sem_inc(s_ohTf[b], -1)
                                v.tensor_scalar(onehotT[:, b, :], dstrow[:, b, :], tnode[:, ds(t, 1)], None,
                                                ALU.is_equal).then_inc(s_ohT, 1)
                        if edge_net:
                            for b in range(2):
                                v.wait_ge(s_seg[b], 1)
                                v.sem_inc(s_seg[b], -1)
                                v.sem_inc(s_rlf[b], 1)
                                make_onehot(c, t, 2 * b)
                                make_onehot(c, t, 2 * b + 1)
                    v.wait_ge(s_acc, 1)
                    v.sem_inc(s_acc, -1)
                    link(v.tensor_copy(pair[:, ds(t, 1), 0:H], ps_acc[:, 0:H]))
                    v.sem_inc(s_accf, 1)

            def gru(k):
                with v.Fori(0, NB) as b:
                    v.tensor_copy(stage[:, :, :], block_of(pair, b))
                    v.tensor_copy(hstage[:, :, :], block_of(h, b)).then_inc(s_stg, 1)
                    v.wait_ge(s_rz, 1)
                    v.sem_inc(s_rz, -1)
                    link(v.tensor_tensor(cand[:, :, :], rz[:, :, 0:H], ps_g[:, :, 3 * H:], ALU.mult))
                    v.tensor_tensor(cand[:, :, :], cand[:, :, :], ps_g[:, :, 2 * H:3 * H], ALU.add).then_inc(s_cd, 1)
                    v.wait_ge(s_th, 1)
                    v.sem_inc(s_th, -1)
                    link(v.tensor_tensor(dif[:, :, :], hstage[:, :, :], cand[:, :, :], ALU.subtract))
                    link(v.tensor_tensor(dif[:, :, :], dif[:, :, :], rz[:, :, H:], ALU.mult))
                    if k == 0:
                        link(v.tensor_tensor(block_of(h, b), dif[:, :, :], cand[:, :, :], ALU.add))
                    else:
                        link(v.tensor_tensor(dif[:, :, :], dif[:, :, :], cand[:, :, :], ALU.add))
                        link(v.tensor_tensor(block_of(x, b), block_of(x, b), dif[:, :, :], ALU.add))

            def dense(check=False):
                for t0, t1 in SPLIT:
                    v.wait_ge(s_sp2, 1)
                    v.sem_inc(s_sp2, -1)
                    v.scalar_tensor_tensor(out=q[:, t0:t1, :], in0=h[:, t0:t1, :], scalar=SCALE,
                                           in1=hsp[:, t0:t1, 0:H], op0=ALU.mult, op1=ALU.subtract).then_inc(s_sp1, 1)
                for t0, t1 in SPLIT:
                    v.wait_ge(s_sp2, 1)
                    v.sem_inc(s_sp2, -1)
                    v.tensor_tensor(q[:, t0:t1, :], q[:, t0:t1, :], hsp[:, t0:t1, H:2 * H],
                                    ALU.subtract).then_inc(s_sp1, 1)
                for _ in SPLIT:
                    v.wait_ge(s_sp2, 1)
                    v.sem_inc(s_sp2, -1)
                v.sem_inc(s_hsp, 1)

                def tile(t, b):
                    v.wait_ge(s_d, 1)
                    v.sem_inc(s_d, -1)
                    if check:
                        link(v.tensor_tensor(ored, ored, amat[b].rearrange("p s d -> p (s d)").bitcast(i32),
                                             ALU.bitwise_or))
                    v.sem_inc(s_alf[b], 1)
                    link(v.tensor_reduce(pair[:, ds(t, 1), 0:H],
                                         ps_d[:, b % 2, 0:3 * H].rearrange("p (k f) -> p f k", k=3), AX, ALU.add))
                    v.sem_inc(s_df, 1)

                with v.Fori(0, NT // 4) as i:
                    for b in range(4):
                        tile(i * 4 + b, b)
                tile(NT - 1, 0)

            def build_tile(t):
                with v.Fori(0, WT // 2) as w:
                    lo0, ng0, lo1, ng1 = load_windows(v, t, w)
                    for i, (lo, ng) in enumerate(((lo0, ng0), (lo1, ng1))):
                        with v.Fori(0, ng) as g:
                            c = first_chunk(v, lo, g, GW)
                            v.wait_ge(s_woh[i], 1)
                            v.sem_inc(s_woh[i], -1)
                            for j in range(GW):
                                v.tensor_scalar(oh_hi[:, i, j, :], iota_h[:, :],
                                                wbase[:, ds(t * WT + w * 2 + i, 1)], key[:, ds(c + j, 1)],
                                                ALU.add, ALU.is_equal)
                                last = v.tensor_scalar(oh_lo[:, i, j, :], iota_h[:, 0:P],
                                                       src_lo[:, ds(c + j, 1)], None, ALU.is_equal)
                            last.then_inc(s_wsem, 1)

            v.wait_ge(s_cst, 1)
            v.wait_ge(s_load, 16 * n_load)
            link(v.tensor_copy(cidx, cidx_i))
            v.tensor_scalar(iota_f[:, :], cidx[:, 0:P], -1.0, None, ALU.add)
            v.tensor_scalar(iota_h[:, :], cidx[:, 0:WC], -1.0, None, ALU.add)
            v.tensor_scalar(wbase, cidx[:, 0:NW], float(WC), float(-WC), ALU.mult, ALU.add)
            v.tensor_scalar(tbase[:, :], cidx[:, 0:NTP], float(P), float(-P), ALU.mult, ALU.add)
            v.tensor_scalar(cidx0[:, :], cidx[:, 0:RBMAX], float(P * GC * RBG), float(-P * GC * RBG), ALU.mult, ALU.add)
            v.tensor_copy(pcol[:, :], pcol_i[:, :])
            v.tensor_copy(rkey, rkey_i)
            link(v.tensor_copy(dst_f[:, :], dst_i))
            v.tensor_reduce(mm13[:, 0, :], dst_cm.rearrange("p (k e) -> p k e", e=P), AX, ALU.min)
            v.tensor_reduce(mm13[:, 1, :], dst_cm.rearrange("p (k e) -> p k e", e=P), AX, ALU.max).then_inc(s_mm, 1)
            sh = cpick.bitcast(i32)
            link(v.tensor_scalar(sh, dst_i, 3, None, ALU.logical_shift_right))
            link(v.tensor_scalar(src_lo, sh, float(WC), None, ALU.mult))
            link(v.tensor_scalar(sh, dst_i, DW - 1, None, ALU.bitwise_and))
            link(v.tensor_tensor(src_lo, src_lo, sh, ALU.add))
            link(v.tensor_scalar(sh, src_i[:, :], 7, None, ALU.logical_shift_right))
            link(v.tensor_scalar(cidx_f, sh, float(DW), None, ALU.mult))
            link(v.tensor_tensor(key, src_lo, cidx_f, ALU.add))
            link(v.tensor_scalar(sh, src_i[:, :], P - 1, None, ALU.bitwise_and))
            link(v.tensor_copy(src_lo, sh))
            link(v.tensor_copy(pw_i[:, 0:1], pcol_i[:, :]))
            link(v.tensor_scalar(pw_i[:, 2:3], pcol_i[:, :], 1, None, ALU.bitwise_and))
            link(v.tensor_copy(lohi[:, 4:5], pw_i[:, 2:3]))
            link(v.tensor_scalar(lohi[:, 5:6], pcol[:, :], float(P // 2 - 1), None, ALU.add))
            link(v.tensor_copy(pw_i[:, 3:4], lohi[:, 5:6]))
            link(v.tensor_scalar(pw_i[:, 1:2], pw_i[:, 3:4], 23, None, ALU.logical_shift_left))
            link(v.tensor_tensor(pw[:, 1:2], pw_i[:, 1:2].bitcast(f32), lohi[:, 4:5], ALU.mult))
            link(v.tensor_tensor(pw[:, 0:1], pw_i[:, 1:2].bitcast(f32), pw[:, 1:2], ALU.subtract))
            v.tensor_scalar(tnode[:, :], tbase[:, :], pcol[:, 0:1], None, ALU.add).then_inc(s_cst2, 1)
            link(v.tensor_scalar(lohi[:, 2:3], pcol[:, :], float(P), None, ALU.mult))
            link(v.tensor_scalar(lohi[:, 3:4], lohi[:, 2:3], float(P - 1), None, ALU.add))
            for k in range(WK):
                last = v.tensor_scalar(wedge[:, 0, k:k + 1], pcol[:, :], float(WK * DW), float(k * DW), ALU.mult, ALU.add)
            link(last)
            link(v.tensor_scalar(wedge[:, 1, :], wedge[:, 0, :], float(DW - 1), None, ALU.add))
            v.wait_ge(s_mmb, 32)
            for k in range(WK):
                link(v.scalar_tensor_tensor(out=cpick, in0=cmin, scalar=wedge[:, 1, k:k + 1], in1=cidx,
                                            op0=ALU.is_le, op1=ALU.mult))
                link(v.reduce_max(wlohi[:, k, 1:2], cpick, AX))
            link(v.scalar_tensor_tensor(out=cpick, in0=cmin, scalar=lohi[:, 3:4], in1=cidx,
                                        op0=ALU.is_le, op1=ALU.mult))
            link(v.reduce_max(lohi[:, 1:2], cpick, AX))
            link(v.tensor_scalar(cidx, cidx, -1.0, float(CHP + 1), ALU.mult, ALU.add))
            for k in range(WK):
                link(v.scalar_tensor_tensor(out=cpick, in0=cmax, scalar=wedge[:, 0, k:k + 1], in1=cidx,
                                            op0=ALU.is_ge, op1=ALU.mult))
                link(v.reduce_max(wlohi[:, k, 0:1], cpick, AX))
            link(v.tensor_scalar(wlohi[:, :, 0], wlohi[:, :, 0], -1.0, float(CHP), ALU.mult, ALU.add))
            v.tensor_scalar(wlohi[:, :, 0], wlohi[:, :, 0], float(CH - 1), None, ALU.min).then_inc(s_wl, 1)
            link(v.scalar_tensor_tensor(out=cpick, in0=cmax, scalar=lohi[:, 2:3], in1=cidx,
                                        op0=ALU.is_ge, op1=ALU.mult))
            link(v.reduce_max(lohi[:, 0:1], cpick, AX))
            link(v.tensor_scalar(lohi[:, 0:1], lohi[:, 0:1], -1.0, float(CHP), ALU.mult, ALU.add))
            v.tensor_scalar(lohi[:, 0:1], lohi[:, 0:1], float(CH - 1), None, ALU.min).then_inc(s_lh, 1)
            v.wait_ge(s_lhr, 16)
            link(v.tensor_tensor(rowf[:, 2, :], rowp[:, :, 1], rowp[:, :, 0], ALU.subtract))
            link(v.tensor_scalar(rowf[:, 2, :], rowf[:, 2, :], 1.0, float(GC - 1), ALU.max, ALU.add))
            link(v.tensor_copy(rowi[:, 2, :], rowf[:, 2, :]))
            link(v.tensor_scalar(rowi[:, 1, :], rowi[:, 2, :], 2, None, ALU.arith_shift_right))
            link(v.tensor_copy(rowf[:, 2, :], rowi[:, 1, :]))
            link(v.tensor_scalar(rowf[:, 3, :], rowf[:, 2, :], float(RBG - 1), None, ALU.add))
            link(v.tensor_copy(rowi[:, 2, :], rowf[:, 3, :]))
            link(v.tensor_scalar(rowi[:, 3, :], rowi[:, 2, :], 4, None, ALU.arith_shift_right))
            link(v.memset(rowf[:, 1, :], 0.0))
            link(v.tensor_tensor_scan(rowf[:, 3, :], rowf[:, 2, :], rowf[:, 1, :], 0.0, ALU.add, ALU.add))
            link(v.memset(tile_tab[:, :, :], 0))
            link(v.tensor_scalar(cidx, cidx, float(-P), float(P * CHP), ALU.mult, ALU.add))
            v.tensor_copy(tile_tab[:, 0:NT, 0], rowp[:, 0:NT, 0])
            v.tensor_copy(tile_tab[:, 0:NT, 1], rowi[:, 1, 0:NT])
            v.tensor_copy(tile_tab[:, 1:NT + 1, 2], rowf[:, 3, 0:NT])
            link(v.tensor_copy(tile_tab[:, 0:NT, 3], rowi[:, 3, 0:NT]))
            v.sem_inc(s_tab, 4)
            link(v.memset(aux[:, :, :], 0.0))
            with v.Fori(0, NT) as t:
                lo, ng, nr = load_range(v, t, (0, 1, 3))
                with v.Fori(0, nr) as r:
                    link(v.tensor_copy(raw[:, ds(r * RBLK, RBLK)], zeros[:, :]))
                v.sem_inc(s_rawz, 1)
                with v.Fori(0, ng) as g:
                    c = first_chunk(v, lo, g)
                    for b in range(2):
                        v.wait_ge(s_seg[b], 1)
                        v.sem_inc(s_seg[b], -1)
                        make_onehot(c, t, 2 * b)
                        make_onehot(c, t, 2 * b + 1)
                v.wait_ge(s_st, 1)
                v.sem_inc(s_st, -1)
                v.tensor_copy(aux[:, ds(t, 1), 0:E16W], ps_m[:, 0:E16W]).then_inc(s_stf, 1)
                v.wait_ge(s_rawc, 1)
                v.sem_inc(s_rawc, -1)
                link(v.memset(rmax[:, 0:1], 0.0))
                with v.Fori(0, nr) as r:
                    link(v.tensor_scalar(rkey_i, raw[:, ds(r * RBLK, RBLK)].bitcast(i32), 23, None,
                                         ALU.logical_shift_right))
                    link(v.tensor_copy(rexp, rkey_i))
                    link(v.tensor_tensor(rsel, rexp, rkey, ALU.add))
                    link(v.tensor_scalar(rsel, rsel, cidx0[:, ds(r, 1)], None, ALU.add))
                    link(v.scalar_tensor_tensor(out=rsel, in0=rexp, scalar=1.0,
                                                in1=rsel, op0=ALU.is_ge, op1=ALU.mult))
                    link(v.reduce_max(rmax[:, 1:2], rsel, AX))
                    link(v.tensor_tensor(rmax[:, 0:1], rmax[:, 0:1], rmax[:, 1:2], ALU.max))
                link(v.tensor_scalar(last_f[:, ds(t, 1)], rmax[:, 0:1], cidx[:, ds(lo, 1)], float(-(P // 2)),
                                     ALU.add, ALU.add))
            v.sem_inc(s_st2, 1)
            link(v.tensor_copy(deg[:, :], aux[:, :, F16]))
            link(v.tensor_scalar(dinv[:, :], deg[:, :], 1.0, None, ALU.add))
            v.reciprocal(dinv[:, :], dinv[:, :]).then_inc(s_sq, 1)
            v.wait_ge(s_sqd, 1)
            v.sem_inc(s_sqd, -1)
            link(v.tensor_scalar(rcnt[:, :], deg[:, :], 1.0, None, ALU.max))
            link(v.reciprocal(rcnt[:, :], rcnt[:, :]))
            link(v.tensor_scalar(has[:, :], deg[:, :], 1.0, None, ALU.min))
            link(v.memset(last_f[:, NT:], 0.0))
            link(v.tensor_tensor(last_f[:, :], last_f[:, :], has[:, :], ALU.mult))
            link(v.tensor_scalar(last_f[:, :], last_f[:, :], 0.0, float(E - 1), ALU.max, ALU.min))
            link(v.tensor_copy(last_i[:, :], last_f[:, :]))
            v.sem_inc(s_last, 1)
            v.wait_ge(s_wlr, 16)
            rw = roww.rearrange("o (w a) -> o w a", a=2)
            link(v.tensor_tensor(rw[:, :, 1], rw[:, :, 1], rw[:, :, 0], ALU.subtract))
            link(v.tensor_scalar(rw[:, :, 1], rw[:, :, 1], 1.0, float(GW - 1), ALU.max, ALU.add))
            link(v.tensor_copy(win_tab[:, :, :], rw))
            link(v.tensor_scalar(win_tab[:, :, 1], win_tab[:, :, 1], 1, None, ALU.arith_shift_right))
            v.sem_inc(s_build, 1)
            with v.Fori(0, NT) as t:
                build_tile(t)
            v.wait_ge(s_lgd, 1)
            v.sem_inc(s_lgd, -1)
            link(v.tensor_tensor(aux[:, :, 32:32 + F16], q[:, :, 0:F16], bc(has[:, :], F16), ALU.mult))
            link(v.tensor_copy(aux[:, :, 48:49], has[:, :].unsqueeze(2)))
            link(v.memset(aux[:, :, 49:50], 1.0))
            with v.Fori(0, NB) as b:
                v.tensor_copy(hstage[:, :, :], block_of(aux, b)).then_inc(s_stg, 1)
                v.wait_ge(s_auxT, 1)
                v.sem_inc(s_auxT, -1)
            v.wait_ge(s_x, 16)
            norm()
            v.sem_inc(s_sp1, 1)
            link(v.memset(ored, 0))
            dense(check=True)
            link(v.tensor_scalar(ored, ored, BIG_BITS, None, ALU.bitwise_and))
            link(v.reduce_max(lohi[:, 6:7], ored, AX))
            v.tensor_scalar(lohi[:, 7:8], lohi[:, 6:7], 1.0, None, ALU.min).then_inc(s_or, 1)
            v.wait_ge(s_flag1, 1)
            v.sem_inc(s_flag1, -1)
            link(v.tensor_scalar(flag[0:1, 0:1], ps_m[0:1, 0:1], 1.0, None, ALU.min))
            v.sem_inc(s_flag, 4)
            v.sem_inc(s_hrdy, 1)
            big = v.value_load(flag[0:1, 0:1], min_val=0, max_val=1)

            def in_sums():
                v.sem_inc(s_hrdy, 1)
                with v.If(big):
                    spread()
                with v.Else():
                    v.sem_inc(s_sp1, 1)
                    dense()

            with v.If(big):
                spread()
            for k in range(2):
                if k == 1:
                    in_sums()
                link(v.tensor_tensor(pair[:, :, H:], h[:, :, :], bc(deg[:, :], H), ALU.mult))
                gru(k)
            norm()
            link(v.tensor_tensor(h[:, :, :], h[:, :, :], bc(dinv[:, :], H), ALU.mult))
            in_sums()
            link(v.tensor_tensor(pair[:, :, 0:H], pair[:, :, 0:H], h[:, :, :], ALU.add))
            link(v.tensor_tensor(pair[:, :, 0:H], pair[:, :, 0:H], bc(dinv[:, :], H), ALU.mult))
            with v.Fori(0, NB) as b:
                v.tensor_copy(stage[:, :, :], block_of(pair, b)).then_inc(s_stg, 1)
                v.wait_ge(s_gt, 1)
                v.sem_inc(s_gt, -1)
                link(v.tensor_tensor(block_of(h, b), ps_g[:, :, 0:H], bc(dinv[:, ds(b * TB, TB)], H), ALU.mult))
            in_sums()
            link(v.tensor_tensor(pair[:, :, 0:H], pair[:, :, 0:H], h[:, :, :], ALU.add))
            link(v.tensor_tensor(pair[:, :, 0:H], pair[:, :, 0:H], bc(dinv[:, :], H), ALU.mult))
            link(v.tensor_tensor(x[:, :, :], x[:, :, :], pair[:, :, 0:H], ALU.add))
            link(v.tensor_tensor(x[:, :, :], x[:, :, :],
                                 W["w_b2r"][:, :].unsqueeze(1).broadcast_to([P, NTP, H]), ALU.add))
            norm()
            in_sums()
            link(v.tensor_copy(pair[:, :, H:], h[:, :, :]))
            link(v.tensor_tensor(pair[:, :, 0:H], pair[:, :, 0:H], bc(rcnt[:, :], H), ALU.mult))
            with v.Fori(0, NB) as b:
                v.tensor_copy(stage[:, :, :], block_of(pair, b)).then_inc(s_stg, 1)
                v.wait_ge(s_gt, 1)
                v.sem_inc(s_gt, -1)
                link(v.tensor_tensor(block_of(x, b), block_of(x, b), ps_g[:, :, 0:H], ALU.add))
            norm()
            with v.Fori(0, NB) as b:
                v.tensor_copy(hstage[:, :, :], block_of(h, b)).then_inc(s_stg, 1)
                v.wait_ge(s_gt, 1)
                v.sem_inc(s_gt, -1)
                v.tensor_copy(block_of(q, b), ps_g[:, :, H:2 * H])
                link(v.tensor_copy(pair[:, ds(b * TB, TB), H:], ps_g[:, :, 0:H]))
            v.sem_inc(s_hrdy, 1)
            spread(True)
            gru(2)
            v.sem_inc(s_out, 1)


def kernel(**inputs):
    import numpy as np
    import concourse.bacc as bacc
    from concourse.bass_utils import run_bass_kernel_spmd

    I = {k: np.asarray(a) for k, a in inputs.items()}

    def edges(a, pad):
        full = np.full((CHP * P,) + a.shape[1:], pad, a.dtype)
        full[:E] = a
        return full

    def put(shape, *parts):
        full = np.zeros(shape, np.float32)
        for r, c, a in parts:
            full[r:r + a.shape[0], c:c + a.shape[1]] = a
        return full

    xp = np.zeros((NTP * P, H), np.float32)
    xp[:N] = I["x"]
    src, dst = edges(I["src"], 0), edges(I["dst"], PAD_DST)
    e16p = np.ones((CHE, P, E16W), np.float32)
    e16p[:, :, :F16] = edges(I["edge_attr_16"], 0).reshape(CHP, P, F16)[:CHE]
    A = {
        "x_nm": xp.reshape(NTP, P, H).transpose(1, 0, 2).reshape(P, NTP * H),
        "srcT": src.reshape(CHP, P).T, "dstT": dst.reshape(CHP, P).T, "dst_lin": dst,
        "e16": I["edge_attr_16"],
        "e16p": e16p.transpose(1, 0, 2).reshape(P, CHE * E16W),
        "e32T": edges(I["edge_attr_32"], 0).T,
    }

    def gates(k, w_ih, w_hh, b_ih, b_hh):
        A[f"w_i{k}"] = put((P, 4 * H), (0, 0, w_ih.T))
        A[f"w_h{k}"] = put((H, 4 * H), (0, 0, w_hh.T[:, :2 * H]), (0, 3 * H, w_hh.T[:, 2 * H:]))
        A[f"w_b{k}"] = put((2, 4 * H), (0, 0, b_ih[None]), (1, 0, b_hh[None, :2 * H]), (1, 3 * H, b_hh[None, 2 * H:]))

    for k in range(2):
        w, b = I["L0_gnn_W_msg"][k], I["L0_gnn_b_msg"][k]
        A[f"w_a{k}"] = put((P, P), (0, 0, w[H:2 * H]), (H, 0, w[:H]))
        A[f"w_x{k}"] = put((H, P), (0, 0, w[2 * H:]), (F16, 0, b[None]))
        gates(k, I["L0_gnn_W_ih"][k], I["L0_gnn_W_hh"][k], I["L0_gnn_b_ih"][k], I["L0_gnn_b_hh"][k])
    A["w_c1"] = put((P, P), (0, 0, I["L1_gnn_W1"]))
    A["w_b1c"] = I["L1_gnn_b1"][:, None]
    A["w_c2"] = I["L1_gnn_W2"]
    A["w_b2r"] = np.broadcast_to(I["L1_gnn_b2"], (P, H))
    A["w_l"] = put((P, P), (0, 0, I["L2_gnn_W_l"]), (H, 0, I["L2_gnn_W_r"]))
    A["w_le"] = put((H, P), (32, 0, I["L2_gnn_W_e"]), (48, 0, I["L2_gnn_b_e"][None]), (49, 0, I["L2_gnn_b_l"][None]))
    w1 = I["L3_gnn_W1"].T
    A["w_pq"] = put((H, P), (0, 0, w1[:H]), (0, H, w1[H:2 * H]))
    A["w_bq"] = put((1, P), (0, H, I["L3_gnn_b1"][None]))
    A["w_e3"] = w1[2 * H:]
    A["w_a2"] = put((P, P), (0, 0, I["L3_gnn_W2"].T))
    A["w_x2"] = put((H, P), (F16, 0, I["L3_gnn_b2"][None]))
    gates(2, I["L3_gnn_w_ih"], I["L3_gnn_w_hh"], I["L3_gnn_b_ih"], I["L3_gnn_b_hh"])
    A = {k: np.ascontiguousarray(a) for k, a in A.items()}

    nc = bacc.Bacc("TRN2", target_bir_lowering=False, num_devices=1)
    D = {k: nc.dram_tensor("in_" + k, a.shape, mybir.dt.from_np(a.dtype), kind="ExternalInput").ap()
         for k, a in A.items()}
    out = nc.dram_tensor("out_nm", (P, NTP * H), f32, kind="ExternalOutput").ap()
    gnn(nc, D, out)
    r = run_bass_kernel_spmd(nc, [{"in_" + k: a for k, a in A.items()}], core_ids=[0])
    got = r.results[0]["out_nm"].reshape(P, NTP, H).transpose(1, 0, 2).reshape(NTP * P, H)
    return np.ascontiguousarray(got[:N])
```
